# Optimizing a Trainium2 kernel written in Bass

```python
import numpy as np
import jax
import jax.numpy as jnp

def _softmax(x, axis=-1):
    return jax.nn.softmax(x, axis=axis)

def _gelu(x):
    return jax.nn.gelu(x, approximate=True)

def _silu(x):
    return jax.nn.silu(x)

def _sigmoid(x):
    return jax.nn.sigmoid(x)

def _layernorm(x, axis=-1, eps=1e-05):
    m = jnp.mean(x, axis=axis, keepdims=True)
    v = jnp.var(x, axis=axis, keepdims=True)
    return (x - m) / jnp.sqrt(v + eps)

def _scatter_add(tgt, idx, src, axis=0):
    return tgt.at[idx].add(src)

def _segment_sum(src, seg, n):
    return jax.ops.segment_sum(src, seg, n)
kernel_name = 'mk_seq_postln_d1_jaxref_r4_37482a'

def setup_inputs(seed: int=0):
    np.random.seed(seed)
    _w = jnp.asarray

    def _L0_attn_setup():
        import jax, jax.numpy as jnp
        import numpy as np
        D_MODEL = 256
        D_STATE = 16
        D_CONV = 4
        EXPAND = 2
        D_INNER = D_MODEL * EXPAND
        BATCH = 2
        SEQ = 256

        def _mamba_forward(x, W_in, conv_w, conv_b, W_xproj, W_dt, b_dt, A_log, Dp, W_out):
            xz = x @ W_in
            x_in, z = jnp.split(xz, 2, axis=-1)
            xc = jnp.transpose(x_in, (0, 2, 1))
            xc = jax.lax.conv_general_dilated(xc, conv_w, window_strides=(1,), padding=[(D_CONV - 1, 0)], feature_group_count=D_INNER, dimension_numbers=('NCH', 'OIH', 'NCH'))
            xc = xc + conv_b[None, :, None]
            xc = jax.nn.silu(jnp.transpose(xc, (0, 2, 1)))
            A = -jnp.exp(A_log)
            xp = xc @ W_xproj
            dt_raw = xp[..., :1]
            B_sel = xp[..., 1:1 + D_STATE]
            C_sel = xp[..., 1 + D_STATE:]
            delta = jax.nn.softplus(dt_raw @ W_dt + b_dt)
            dA = jnp.exp(delta[..., None] * A)
            dBx = (delta * xc)[..., None] * B_sel[:, :, None, :]

            def step(h, inp):
                dA_t, dBx_t, C_t = inp
                h = dA_t * h + dBx_t
                y_t = jnp.einsum('bdn,bn->bd', h, C_t)
                return (h, y_t)
            h0 = jnp.zeros((x.shape[0], D_INNER, D_STATE), xc.dtype)
            _, ys = jax.lax.scan(step, h0, (dA.swapaxes(0, 1), dBx.swapaxes(0, 1), C_sel.swapaxes(0, 1)))
            y = ys.swapaxes(0, 1) + Dp * xc
            y = y * jax.nn.silu(z)
            return y @ W_out
        key = jax.random.key(seed)
        ks = jax.random.split(key, 9)
        s = lambda fan: 1.0 / np.sqrt(fan)
        x = jax.random.normal(ks[0], (BATCH, SEQ, D_MODEL), jnp.float32)
        W_in = jax.random.normal(ks[1], (D_MODEL, 2 * D_INNER), jnp.float32) * s(D_MODEL)
        conv_w = jax.random.normal(ks[2], (D_INNER, 1, D_CONV), jnp.float32) * s(D_CONV)
        conv_b = jax.random.normal(ks[3], (D_INNER,), jnp.float32) * 0.01
        W_xproj = jax.random.normal(ks[4], (D_INNER, 2 * D_STATE + 1), jnp.float32) * s(D_INNER)
        W_dt = jax.random.normal(ks[5], (1, D_INNER), jnp.float32)
        dt_std = 1.0 / np.sqrt(D_INNER)
        b_dt = jax.random.uniform(ks[6], (D_INNER,), jnp.float32, minval=-dt_std, maxval=dt_std)
        A_log = jnp.log(jnp.arange(1, D_STATE + 1, dtype=jnp.float32))
        Dp = jnp.ones((D_INNER,), jnp.float32)
        W_out = jax.random.normal(ks[7], (D_INNER, D_MODEL), jnp.float32) * s(D_INNER)
        return dict(x=x, W_in=W_in, conv_w=conv_w, conv_b=conv_b, W_xproj=W_xproj, W_dt=W_dt, b_dt=b_dt, A_log=A_log, Dp=Dp, W_out=W_out)
    _L0_attn_in = _L0_attn_setup()

    def _L0_ffn_setup():
        import jax, jax.numpy as jnp
        import numpy as np
        D_MODEL, D_FF, N_EXPERTS, TOP_K = (256, 512, 8, 2)
        B, S = (2, 512)
        key = jax.random.key(seed)
        ks = jax.random.split(key, 6)
        sd = 1.0 / np.sqrt(D_MODEL)
        sf = 1.0 / np.sqrt(D_FF)
        return {'x': jax.random.normal(ks[0], (B, S, D_MODEL), jnp.float32), 'router_w': jax.random.normal(ks[1], (N_EXPERTS, D_MODEL), jnp.float32) * sd, 'gate_w': jax.random.normal(ks[2], (N_EXPERTS, D_MODEL, D_FF), jnp.float32) * sd, 'gate_b': jnp.zeros((N_EXPERTS, D_FF), jnp.float32), 'up_w': jax.random.normal(ks[3], (N_EXPERTS, D_MODEL, D_FF), jnp.float32) * sd, 'up_b': jnp.zeros((N_EXPERTS, D_FF), jnp.float32), 'down_w': jax.random.normal(ks[4], (N_EXPERTS, D_FF, D_MODEL), jnp.float32) * sf, 'down_b': jnp.zeros((N_EXPERTS, D_MODEL), jnp.float32)}
    _L0_ffn_in = _L0_ffn_setup()
    _d = {'L0_attn_x': _L0_attn_in['x'], 'L0_attn_W_in': _L0_attn_in['W_in'], 'L0_attn_conv_w': _L0_attn_in['conv_w'], 'L0_attn_conv_b': _L0_attn_in['conv_b'], 'L0_attn_W_xproj': _L0_attn_in['W_xproj'], 'L0_attn_W_dt': _L0_attn_in['W_dt'], 'L0_attn_b_dt': _L0_attn_in['b_dt'], 'L0_attn_A_log': _L0_attn_in['A_log'], 'L0_attn_Dp': _L0_attn_in['Dp'], 'L0_attn_W_out': _L0_attn_in['W_out'], 'L0_ffn_router_w': _L0_ffn_in['router_w'], 'L0_ffn_gate_w': _L0_ffn_in['gate_w'], 'L0_ffn_gate_b': _L0_ffn_in['gate_b'], 'L0_ffn_up_w': _L0_ffn_in['up_w'], 'L0_ffn_up_b': _L0_ffn_in['up_b'], 'L0_ffn_down_w': _L0_ffn_in['down_w'], 'L0_ffn_down_b': _L0_ffn_in['down_b']}
    _x0 = _d['L0_attn_x']
    _d['L0_attn_x'] = jax.random.normal(jax.random.fold_in(jax.random.key(seed), 1), (8, 512, 256), dtype=_x0.dtype)
    del _x0
    return _d

def reference(L0_attn_x, L0_attn_W_in, L0_attn_conv_w, L0_attn_conv_b, L0_attn_W_xproj, L0_attn_W_dt, L0_attn_b_dt, L0_attn_A_log, L0_attn_Dp, L0_attn_W_out, L0_ffn_router_w, L0_ffn_gate_w, L0_ffn_gate_b, L0_ffn_up_w, L0_ffn_up_b, L0_ffn_down_w, L0_ffn_down_b):

    def _L0_attn_ref(x, W_in, conv_w, conv_b, W_xproj, W_dt, b_dt, A_log, Dp, W_out):
        import jax, jax.numpy as jnp
        import numpy as np
        D_MODEL = 256
        D_STATE = 16
        D_CONV = 4
        EXPAND = 2
        D_INNER = D_MODEL * EXPAND
        BATCH = 2
        SEQ = 256

        def _mamba_forward(x, W_in, conv_w, conv_b, W_xproj, W_dt, b_dt, A_log, Dp, W_out):
            xz = x @ W_in
            x_in, z = jnp.split(xz, 2, axis=-1)
            xc = jnp.transpose(x_in, (0, 2, 1))
            xc = jax.lax.conv_general_dilated(xc, conv_w, window_strides=(1,), padding=[(D_CONV - 1, 0)], feature_group_count=D_INNER, dimension_numbers=('NCH', 'OIH', 'NCH'))
            xc = xc + conv_b[None, :, None]
            xc = jax.nn.silu(jnp.transpose(xc, (0, 2, 1)))
            A = -jnp.exp(A_log)
            xp = xc @ W_xproj
            dt_raw = xp[..., :1]
            B_sel = xp[..., 1:1 + D_STATE]
            C_sel = xp[..., 1 + D_STATE:]
            delta = jax.nn.softplus(dt_raw @ W_dt + b_dt)
            dA = jnp.exp(delta[..., None] * A)
            dBx = (delta * xc)[..., None] * B_sel[:, :, None, :]

            def step(h, inp):
                dA_t, dBx_t, C_t = inp
                h = dA_t * h + dBx_t
                y_t = jnp.einsum('bdn,bn->bd', h, C_t)
                return (h, y_t)
            h0 = jnp.zeros((x.shape[0], D_INNER, D_STATE), xc.dtype)
            _, ys = jax.lax.scan(step, h0, (dA.swapaxes(0, 1), dBx.swapaxes(0, 1), C_sel.swapaxes(0, 1)))
            y = ys.swapaxes(0, 1) + Dp * xc
            y = y * jax.nn.silu(z)
            return y @ W_out
        return _mamba_forward(x, W_in, conv_w, conv_b, W_xproj, W_dt, b_dt, A_log, Dp, W_out)

    def _L0_ffn_ref(x, router_w, gate_w, gate_b, up_w, up_b, down_w, down_b):
        import jax, jax.numpy as jnp
        import numpy as np
        D_MODEL, D_FF, N_EXPERTS, TOP_K = (256, 512, 8, 2)
        B, S = (2, 512)
        b, s, d = x.shape
        xf = x.reshape(b * s, d)
        n = xf.shape[0]
        router_logits = xf @ router_w.T
        probs = jax.nn.softmax(router_logits, axis=-1)
        topv, topi = jax.lax.top_k(probs, TOP_K)
        mask = jnp.zeros_like(probs).at[jnp.arange(n)[:, None], topi].set(1.0)
        probs = probs * mask
        probs = probs / (probs.sum(axis=-1, keepdims=True) + 1e-09)
        g = jnp.einsum('nd,edf->nef', xf, gate_w) + gate_b
        u = jnp.einsum('nd,edf->nef', xf, up_w) + up_b
        h = jax.nn.silu(g) * u
        expert_out = jnp.einsum('nef,efd->ned', h, down_w) + down_b
        y = jnp.einsum('ne,ned->nd', probs, expert_out)
        return y.reshape(b, s, d)
    x = L0_attn_x
    x = _layernorm(x + _L0_attn_ref(x, L0_attn_W_in, L0_attn_conv_w, L0_attn_conv_b, L0_attn_W_xproj, L0_attn_W_dt, L0_attn_b_dt, L0_attn_A_log, L0_attn_Dp, L0_attn_W_out), axis=-1)
    x = _layernorm(x + _L0_ffn_ref(x, L0_ffn_router_w, L0_ffn_gate_w, L0_ffn_gate_b, L0_ffn_up_w, L0_ffn_up_b, L0_ffn_down_w, L0_ffn_down_b), axis=-1)
    return x

_drawn_inputs = setup_inputs


def setup_inputs(seed=0):
    import zlib

    import numpy as np

    out = dict(_drawn_inputs(seed))
    spreads = {'L0_attn_Dp': (1.0, 0.2),
     'L0_ffn_gate_b': (0.0, 0.1),
     'L0_ffn_up_b': (0.0, 0.1),
     'L0_ffn_down_b': (0.0, 0.1)}
    factors = {'L0_attn_b_dt': 2.685}
    for name, (base, spread) in spreads.items():
        noise = np.random.default_rng([zlib.crc32(name.encode()), seed]).standard_normal(out[name].shape)
        drawn = base * np.exp(spread * noise) if base else spread * noise
        out[name] = jnp.asarray(drawn.astype(out[name].dtype))
    for name, factor in factors.items():
        out[name] = (out[name] * factor).astype(out[name].dtype)
    return out
```

```python
from contextlib import ExitStack

import concourse.bass as bass
from concourse import mybir

ALU = mybir.AluOpType
ACT = mybir.ActivationFunctionType
F32 = mybir.dt.float32
BF16 = mybir.dt.bfloat16
I32 = mybir.dt.int32
U32 = mybir.dt.uint32
X = mybir.AxisListType.X

P = 128
SEQS, T, DM = 8, 512, 256
DI, N, TAPS = 512, 16, 4
E, FF = 8, 512
TB = T // P
DT = DI // P
KM = DM // P
FB = FF // P
TILES = SEQS * TB
TOK = SEQS * T
RING = 4
BG = 4
REGION = TOK + P
DUMP = E * REGION
BLOCKS = 2 * TOK // P + E - 1
BLOCKS += BLOCKS % 2
SPARE = BLOCKS - 2 * TOK // P
EPS = 1e-5
NB = E * (2 * FF + DM)

USES = [
    ("g0", "back", 0, 1), ("g1", "back", 1, 1), ("g2", "back", 0, 2), ("g3", "back", 1, 2),
    ("xt0", "front", 0, 3), ("xt1", "front", 1, 3), ("o0", "back", 0, 4), ("o1", "back", 1, 4),
    ("in0", "front", 0, 5), ("in1", "front", 1, 5), ("in2", "front", 0, 6), ("in3", "front", 1, 6),
    ("rt0", "back", 0, 7), ("rt1", "back", 1, 7), ("z0", "front", 0, 8), ("z1", "front", 1, 8),
    ("dt", "front", 0, 9), ("b", "front", 1, 9), ("lg", "back", 0, 10), ("c", "front", 1, 10),
    ("z2", "front", 0, 11), ("z3", "front", 1, 11), ("d0", "front", 1, 12), ("d1", "front", 0, 12),
    ("pf", "back", 0, 13), ("d2", "front", 1, 13), ("d3", "front", 1, 14),
]
BANK = {name: bank for name, _, bank, _ in USES}
STEP = {name: step for name, _, _, step in USES}
PER = {(kind, b): sum(k == kind and bank == b for _, k, bank, _ in USES) for kind in ("front", "back") for b in (0, 1)}


def fills_before(name, s):
    b = BANK[name]
    at = [u[0] for u in USES].index(name)
    peeled = isinstance(s, int)
    kinds = [k for k, there in (("back", not peeled or s >= 1), ("front", not peeled or s <= SEQS - 2)) if there]
    here = sum(k in kinds and bank == b for _, k, bank, _ in USES[:at])
    if peeled:
        return PER["front", b] * min(s + 1, SEQS) + PER["back", b] * max(s - 1, 0) + here
    return (PER["front", b] + PER["back", b]) * s + (PER["front", b] - PER["back", b] + here)


def mamba_moe_program(nc, x, W_in, conv_w, conv_b, W_xproj, W_dt, b_dt, A_log, Dp, W_out,
                      router_w, gate_w, gate_b, up_w, up_b, down_w, down_b, out):
    x_rows = x.rearrange("s (b p) m -> s p b m", p=P)
    out_rows = out.rearrange("s (b p) m -> s p b m", p=P)
    xn_dram = nc.dram_tensor("xn_scratch", (SEQS, P, TB, DM), F32).ap()
    b_dram = nc.dram_tensor("b_scratch", (2, N, T), F32).ap()
    xs_dram = nc.dram_tensor("expert_in", (DUMP + SPARE * P, DM), F32).ap()
    ys_dram = nc.dram_tensor("expert_out", (BLOCKS * P, DM), F32).ap()
    route_dram = nc.dram_tensor("route_scratch", (SEQS, P, 4 * TB), F32).ap()
    bias_dram = nc.dram_tensor("bias_scratch", (3, NB), BF16).ap()

    with ExitStack() as ctx:
        def sb(name, shape, dt=F32):
            return ctx.enter_context(nc.sbuf_tensor(name, shape, dt))

        def ps(name, shape, dt=F32):
            return ctx.enter_context(nc.psum_tensor(name, shape, dt))

        def sem(name):
            return ctx.enter_context(nc.semaphore(name))

        ident = sb("ident", [P, P])
        before = sb("before", [P, P])
        ones = sb("ones", [P, P])
        w_in = sb("w_in", [P, KM, 2 * DI])
        w_out = sb("w_out", [P, DT, DM])
        w_x = sb("w_x", [P, DT, 2 * N + 1])
        w_rt = sb("w_rt", [P, KM, E])
        w_dtrep = sb("w_dtrep", [P, DT, P])
        diag_d = sb("diag_d", [P, DT, P])
        cw = sb("cw", [P, DT, TAPS])
        cb = sb("cb", [P, DT])
        wdt = sb("wdt", [P, DT])
        bdt = sb("bdt", [P, DT])
        dp = sb("dp", [P, DT])
        a_neg = sb("a_neg", [P, N])
        minus_half = sb("minus_half", [P, TB])
        x_sb = sb("x_sb", [P, TB, DM])
        x_res = sb("x_res", [P, TB, DM])
        xT = sb("xT", [P, KM, T])
        xc = sb("xc", [P, DT, T])
        dtr = sb("dtr", [P, T])
        big = sb("big", [P, 3 * E * KM * FF])
        per = RING * DT * T
        state = big[:, 0:per].rearrange("p (r d t) -> p r d t", r=RING, d=DT)
        b_bc = big[:, per:2 * per].rearrange("p (n t) -> p n t", n=N)
        delta = big[:, 2 * per:5 * per // 2].rearrange("p (q d t) -> p q d t", q=2, d=DT)
        du = big[:, 5 * per // 2:3 * per].rearrange("p (q d t) -> p q d t", q=2, d=DT)
        mid = sb("mid", [P, 4 * TB * DI])
        zs = mid[:, 0:2 * TB * DI].rearrange("p (q b n) -> p q b n", q=2, b=TB)
        y = mid[:, 2 * TB * DI:].rearrange("p (q b n) -> p q b n", q=2, b=TB)
        c_sb = sb("c_sb", [P, 2, TB, N])
        b_sb = sb("b_sb", [N, T])
        gT = sb("gT", [P, TB, DT, P])
        res = sb("res", [P, TB, DM])
        xn = sb("xn", [P, TB, DM])
        xnT = sb("xnT", [P, KM, T])
        stats = sb("stats", [P, TB, 6])
        mean2 = sb("mean2", [P, TB])
        mean = sb("mean", [P, TB])
        apart = sb("apart", [P, TB])
        squares = sb("squares", [P, TB])
        veps = sb("veps", [P, TB])
        rstd = sb("rstd", [P, TB])
        falling = sb("falling", [P, 1, E])
        region0 = sb("region0", [P, 1, E])
        shifted = sb("shifted", [P, TB, E])
        prob = sb("prob", [P, TB, E])
        equal = sb("equal", [P, TB, E])
        pick = sb("pick", [P, 2, TB, E])
        both = sb("both", [P, TB, E])
        base = sb("base", [P, TB + 1, E])
        row_of = sb("row_of", [P, TB, E])
        top = sb("top", [P, 8, TB, 1])
        rows_f = sb("rows_f", [P, 2, TB])
        route = sb("route", [P, 4, TB])
        route_rows = route[:, 0:2].bitcast(U32)
        zeros = sb("zeros", [P, 1, DM])
        bias_f = sb("bias_f", [NB // P, 2, P])
        bias_h = sb("bias_h", [NB // P, 3, P], BF16)
        blocks = sb("blocks", [P, 6, 1, E])
        used_i = sb("used_i", [P, 1, E], I32)
        ends_i = sb("ends_i", [P, 1, E], I32)
        number = sb("number", [P, BLOCKS, 1])
        inside = sb("inside", [P, 2, BLOCKS, E])
        sums = sb("sums", [P, 4, BLOCKS])
        table = sb("table", [P, 3, BLOCKS], I32)

        w_gate = big[:, 0:E * KM * FF].rearrange("p (e k f) -> p e k f", e=E, k=KM)
        w_up = big[:, E * KM * FF:2 * E * KM * FF].rearrange("p (e k f) -> p e k f", e=E, k=KM)
        w_down = big[:, 2 * E * KM * FF:].rearrange("p (e k m) -> p e k m", e=E, k=FB)
        bias_w = mid[0:3, 0:NB // 2].bitcast(BF16)
        g_bias = bias_w[:, 0:E * FF].rearrange("p (e f) -> p e f", e=E)
        u_bias = bias_w[:, E * FF:2 * E * FF].rearrange("p (e f) -> p e f", e=E)
        d_bias = bias_w[:, 2 * E * FF:].rearrange("p (e m) -> p e m", e=E)
        free = NB // 2
        xs = mid[:, free:free + 2 * DM].rearrange("p (k m) -> p k m", k=2)
        xsT = mid[:, free + 512:free + 1024].rearrange("p (k c t) -> p k c t", k=2, c=KM)
        gate_act = mid[:, free + 1024:free + 2048].rearrange("p (k f) -> p k f", k=2)
        hid = mid[:, free + 2048:free + 3072].rearrange("p (k f) -> p k f", k=2)
        hidT = gT[:, 0:2]
        ys = xc[:, 0].rearrange("p (k m) -> p k m", k=2)
        routes = xc[:, 1, 0:SEQS * 4 * TB].rearrange("p (s c b) -> p s c b", s=SEQS, c=4)
        routes_flat = xc[:, 1, 0:SEQS * 4 * TB].rearrange("p (s c) -> p s c", s=SEQS)
        rows_f2 = xc[:, 2, 0:SEQS * 2 * TB].rearrange("p (s c b) -> p s c b", s=SEQS, c=2)
        rows_out = xc[:, 3, 0:SEQS * 2 * TB].bitcast(U32).rearrange("p (s c b) -> p s c b", s=SEQS, c=2)
        outs = mid[:, 0:2 * TB * DM].rearrange("p (k b m) -> p k b m", k=2, b=TB)
        fetched = mid[:, 2 * TB * DM:6 * TB * DM].rearrange("p (k c b m) -> p k c b m", k=2, c=2, b=TB)
        resid = mid[:, 6 * TB * DM:].rearrange("p (k b m) -> p k b m", k=2, b=TB)
        bf_ones = sb("bf_ones", [3, P], BF16)

        psum = ps("psum", [P, 8, 512])
        dA = psum[:, 0:4].rearrange("p (h d) t -> p h d t", h=2)
        hT = psum[:, 4:6]
        ms = psum[:, 6:8]

        par_in = sem("par_in")
        consts = sem("consts")
        prep_act = sem("prep_act")
        prep_dve = sem("prep_dve")
        x_in = sem("x_in")
        x_res_in = sem("x_res_in")
        da_ready = sem("da_ready")
        input_ready = sem("input_ready")
        scanned = sem("scanned")
        ht_ready = sem("ht_ready")
        y_added = sem("y_added")
        filled = [sem(f"filled{b}") for b in range(2)]
        freed = [sem(f"freed{b}") for b in range(2)]
        conv_first = sem("conv_first")
        conv_chain = sem("conv_chain")
        silu_done = sem("silu_done")
        sp_chain = sem("sp_chain")
        delta_done = sem("delta_done")
        du_done = sem("du_done")
        b_stored = [sem(f"b_stored{i}") for i in range(2)]
        b_in = [sem(f"b_in{g}") for g in range(N // BG)]
        gated = sem("gated")
        ln_chain = sem("ln_chain")
        rstd_done = sem("rstd_done")
        xn_done = sem("xn_done")
        stored = sem("stored")
        route_chain = sem("route_chain")
        exp_done = sem("exp_done")
        counted = sem("counted")
        scattered = sem("scattered")
        bias_in = sem("bias_in")
        bias_chain = sem("bias_chain")
        bias_stored = sem("bias_stored")
        table_chain = sem("table_chain")
        zeroed = sem("zeroed")
        w_loaded = sem("w_loaded")
        xs_in = [sem(f"xs_in{k}") for k in range(2)]
        xs_turned = sem("xs_turned")
        xs_copied = sem("xs_copied")
        gate_ready = sem("gate_ready")
        up_ready = sem("up_ready")
        gate_acted = sem("gate_acted")
        hid_ready = sem("hid_ready")
        hid_turned = sem("hid_turned")
        hid_copied = sem("hid_copied")
        down_ready = sem("down_ready")
        ys_copied = sem("ys_copied")
        ys_out = [sem(f"ys_out{k}") for k in range(2)]
        route_in = sem("route_in")
        resid_in = [sem(f"resid_in{k}") for k in range(2)]
        fetched_in = [sem(f"fetched_in{k}") for k in range(2)]
        summed = sem("summed")
        ln2_chain = sem("ln2_chain")
        rstd2_done = sem("rstd2_done")
        normed = sem("normed")
        out_stored = [sem(f"out_stored{k}") for k in range(2)]

        HALVES, PIECES = 2 * N, TB * N
        SPC = 2 * DT + 2
        RC1, RC2, RC3 = 1, 15, TB + 11
        RC = RC1 + RC2 + RC3
        TC = 29
        LN = TB + 7

        block = ctx.enter_context(nc.Block())

        def wait_copied(eng, name, s):
            eng.wait_ge(freed[BANK[name]], fills_before(name, s) + 1)

        FIRST = 3

        def block_loop(eng, step):
            with eng.Fori(0, (BLOCKS - 1 - FIRST) // 2) as i:
                for k in range(2):
                    step(2 * i + (FIRST + k), (FIRST + k) % 2)

        def sequences(eng, body):
            body(0, 0, False, True)
            with eng.Fori(0, (SEQS - 2) // 2) as i:
                for k in range(2):
                    body(2 * i + (1 + k), (1 + k) % 2, True, True)
            body(SEQS - 1, (SEQS - 1) % 2, True, False)

        @block.sync
        def _(sp):
            loads = [
                (w_in[:], W_in.rearrange("(k p) n -> p k n", p=P)),
                (w_out[:], W_out.rearrange("(k p) n -> p k n", p=P)),
                (w_x[:], W_xproj.rearrange("(k p) n -> p k n", p=P)),
                (cw[:], conv_w.rearrange("(k p) o t -> p k (o t)", p=P)),
                (cb[:], conv_b.rearrange("(k p) -> p k", p=P)),
                (wdt[:], W_dt.rearrange("o (k p) -> p (o k)", p=P)),
                (bdt[:], b_dt.rearrange("(k p) -> p k", p=P)),
                (dp[:], Dp.rearrange("(k p) -> p k", p=P)),
                (w_rt[:, 0], router_w[:, 0:P].rearrange("e p -> p e")),
                (w_rt[:, 1], router_w[:, P:DM].rearrange("e p -> p e")),
                (a_neg[:], A_log.rearrange("(o n) -> o n", o=1).to_broadcast([P, N])),
            ]
            sp.dma_start(x_sb[:], x_rows[0]).then_inc(x_in, 16)
            for dst, src in loads:
                sp.dma_start(dst, src, allow_slow_non_contiguous=True).then_inc(par_in, 16)

            def body(s, par, back, front):
                q = 1 - par
                if back:
                    sp.wait_ge(stored, 32 * (s - 1) + 16)
                    sp.dma_start(x_res[:], x_rows[s - 1]).then_inc(x_res_in, 16)
                if front:
                    sp.wait_ge(input_ready, N * s + 1)
                    sp.dma_start(x_sb[:], x_rows[s + 1]).then_inc(x_in, 16)
                if back:
                    sp.wait_ge(xn_done, TB * s)
                    sp.dma_start(xn_dram[s - 1], xn[:]).then_inc(stored, 16)
                if front:
                    wait_copied(sp, "b", s)
                    sp.dma_start(b_dram[q], b_sb[:]).then_inc(b_stored[q], 16)
                    for g in range(N // BG):
                        sp.wait_ge(input_ready, N * s + BG * (g + 1))
                        if g == 0:
                            sp.wait_ge(b_stored[q], 16 * ((s + 1) // 2 + 1) if isinstance(s, int) else 8 * (s + 3 - q))
                        sp.dma_start(b_bc[:, BG * g:BG * (g + 1)], b_dram[q, BG * g:BG * (g + 1)]
                                     .rearrange("(o n) t -> o n t", o=1).to_broadcast([P, BG, T])).then_inc(b_in[g], 16)
                if back:
                    sp.wait_ge(route_chain, RC * s)
                    sp.dma_start(route_dram[s - 1], route[:].rearrange("p c b -> p (c b)")).then_inc(stored, 16)

            for at, src in ((0, gate_b), (E * FF // P, up_b), (2 * E * FF // P, down_b)):
                rows = src.rearrange("e (f c) -> (e f) c", c=P)
                sp.dma_start(bias_f[at:at + rows.shape[0], 0], rows).then_inc(bias_in, 16)
            sp.wait_ge(consts, 9)
            half = SPARE // 2
            sp.dma_start(xs_dram[DUMP:DUMP + half * P].rearrange("(r p) m -> p r m", p=P),
                         zeros[:].to_broadcast([P, half, DM])).then_inc(stored, 16)
            sp.wait_ge(bias_chain, 5)
            sp.dma_start(bias_dram.rearrange("j (r c) -> r j c", c=P), bias_h[:]).then_inc(bias_stored, 16)
            wait_copied(sp, "b", -1)
            sp.dma_start(b_dram[0], b_sb[:]).then_inc(b_stored[0], 16)
            sp.wait_ge(b_stored[0], 16)
            for g in range(N // BG):
                sp.dma_start(b_bc[:, BG * g:BG * (g + 1)], b_dram[0, BG * g:BG * (g + 1)]
                             .rearrange("(o n) t -> o n t", o=1).to_broadcast([P, BG, T])).then_inc(b_in[g], 16)
            sequences(sp, body)
            body(SEQS, 0, True, False)

            sp.wait_ge(ht_ready, PIECES * SEQS)
            sp.dma_start(w_gate, gate_w.rearrange("e (k p) f -> p e k f", p=P)).then_inc(w_loaded, 16)
            sp.dma_start(w_up, up_w.rearrange("e (k p) f -> p e k f", p=P)).then_inc(w_loaded, 16)
            sp.dma_start(w_down, down_w.rearrange("e (k p) m -> p e k m", p=P)).then_inc(w_loaded, 16)
            sp.wait_ge(stored, 32 * SEQS + 16)
            sp.dma_start(routes_flat, route_dram.rearrange("s p c -> p s c")).then_inc(route_in, 16)
            sp.wait_ge(bias_stored, 16)
            sp.dma_start(bias_w, bias_dram).then_inc(w_loaded, 16)
            sp.wait_ge(scattered, 16 + 16 * 2 * TILES)
            sp.wait_ge(table_chain, TC)
            for e in range(E):
                end = sp.value_load(ends_i[0:1, 0, e:e + 1], min_val=0, max_val=DUMP)
                sp.dma_start(xs_dram[bass.ds(end, P)], zeros[:, 0]).then_inc(zeroed, 16)
            sp.wait_ge(zeroed, 16 * E)

            def load_block(j, k):
                if not (isinstance(j, int) and j < 2):
                    sp.wait_ge(xs_turned, j - 1)
                row = sp.value_load(table[0:1, 0, bass.ds(j, 1)], min_val=0, max_val=DUMP + (SPARE - 1) * P)
                sp.dma_start(xs[:, k], xs_dram[bass.ds(row, P)]).then_inc(xs_in[k], 16)

            def store_block(j, k):
                row = sp.value_load(table[0:1, 2, bass.ds(j, 1)], min_val=0, max_val=(BLOCKS - 1) * P)
                sp.wait_ge(ys_copied, j + 1)
                sp.dma_start(ys_dram[bass.ds(row, P)], ys[:, k]).then_inc(ys_out[k], 16)

            for j in range(FIRST + 1):
                load_block(j, j % 2)
            store_block(0, 0)
            block_loop(sp, lambda j, k: (load_block(j + 1, 1 - k), store_block(j - 2, k)))
            for j in range(BLOCKS - 3, BLOCKS):
                store_block(j, j % 2)
            for k in range(2):
                sp.wait_ge(ys_out[k], 16 * (BLOCKS // 2))

            def fetch(s, k):
                if not (isinstance(s, int) and s < 2):
                    sp.wait_ge(normed, TB * (s - 1))
                sp.dma_start(resid[:, k], xn_dram[s]).then_inc(resid_in[k], 16)

            def give(s, k):
                sp.wait_ge(normed, TB * (s + 1))
                sp.dma_start(out_rows[s], outs[:, k]).then_inc(out_stored[k], 16)

            for s in range(2):
                fetch(s, s)
            for s in range(SEQS):
                give(s, s % 2)
                if s + 2 < SEQS:
                    fetch(s + 2, s % 2)
            for k in range(2):
                sp.wait_ge(out_stored[k], 16 * (SEQS // 2))

        @block.gpsimd
        def _(pool):
            pool.memset(ident[:], 0.0).then_inc(consts, 1)
            pool.memset(ones[:], 1.0).then_inc(consts, 1)
            pool.memset(minus_half[:], -0.5).then_inc(consts, 1)
            pool.memset(zeros[:], 0.0).then_inc(consts, 1)
            pool.memset(bf_ones[:], 1.0).then_inc(consts, 1)
            pool.iota(falling[:, 0], pattern=[[-1, E]], base=E, channel_multiplier=0,
                      allow_small_or_imprecise_dtypes=True).then_inc(consts, 1)
            pool.iota(blocks[:, 5, 0], pattern=[[1, E]], base=0, channel_multiplier=0,
                      allow_small_or_imprecise_dtypes=True).then_inc(consts, 1)
            pool.iota(region0[:, 0], pattern=[[REGION, E]], base=0, channel_multiplier=0,
                      allow_small_or_imprecise_dtypes=True).then_inc(consts, 1)
            pool.iota(number[:, :, 0], pattern=[[1, BLOCKS]], base=0, channel_multiplier=0,
                      allow_small_or_imprecise_dtypes=True).then_inc(consts, 1)
            pool.wait_ge(consts, 9)
            pool.affine_select(out=ident[:], in_=ident[:], compare_op=ALU.not_equal, fill=1.0, base=0,
                               pattern=[[-1, P]], channel_multiplier=1).then_inc(consts, 1)
            pool.affine_select(out=before[:], in_=ones[:], compare_op=ALU.is_gt, fill=0.0, base=0,
                               pattern=[[1, P]], channel_multiplier=-1).then_inc(consts, 1)

            pool.wait_ge(consts, 11)
            half = SPARE // 2
            pool.dma_start(xs_dram[DUMP + half * P:DUMP + 2 * half * P].rearrange("(r p) m -> p r m", p=P),
                           zeros[:].to_broadcast([P, half, DM])).then_inc(scattered, 16)

            def step_size(s, q):
                pool.wait_ge(sp_chain, SPC * (s + 1))
                pool.tensor_tensor(delta[:, q], delta[:, q], du[:, q], ALU.add).then_inc(delta_done, 1)
                pool.wait_ge(delta_done, s + 1)
                pool.wait_ge(silu_done, DT * (s + 1))
                pool.tensor_tensor(du[:, q], delta[:, q], xc[:], ALU.mult).then_inc(du_done, 1)

            def rsqrt(s):
                pool.wait_ge(ln_chain, LN * (s + 1))
                pool.tensor_tensor(rstd[:], veps[:], minus_half[:], ALU.pow).then_inc(rstd_done, 1)

            def scatter(s):
                for k in range(2):
                    for b in range(TB):
                        pool.indirect_dma_start(xs_dram, bass.IndirectOffsetOnAxis(ap=route_rows[:, k, b:b + 1], axis=0),
                                                xn[:, b], None).then_inc(scattered, 16)

            def body(s, par, back, front):
                for n in range(N):
                    if n % BG == 0:
                        pool.wait_ge(b_in[n // BG], 16 * (s + 1))
                    if n == 0:
                        pool.wait_ge(du_done, s + 1)
                    if n >= RING or not isinstance(s, int) or s > 0:
                        pool.wait_ge(ht_ready, PIECES * s + TB * (n - RING + 1))
                    pool.tensor_tensor(state[:, n % RING], du[:, par], b_bc[:, n:n + 1].to_broadcast([P, DT, T]),
                                       ALU.mult).then_inc(input_ready, 1)
                    if back and n == 3:
                        pool.wait_ge(y_added, PIECES * s)
                        pool.tensor_tensor(y[:, 1 - par], y[:, 1 - par], zs[:, 1 - par], ALU.mult).then_inc(gated, 1)
                    if back and n == 8:
                        pool.wait_ge(scattered, 16 + 16 * 2 * TB * (s - 1))
                        rsqrt(s - 1)
                if back:
                    pool.wait_ge(route_chain, RC * s)
                if front:
                    step_size(s + 1, 1 - par)
                if back:
                    scatter(s - 1)

            step_size(0, 0)
            sequences(pool, body)
            pool.wait_ge(y_added, PIECES * SEQS)
            q = (SEQS - 1) % 2
            pool.tensor_tensor(y[:, q], y[:, q], zs[:, q], ALU.mult).then_inc(gated, 1)
            pool.wait_ge(scattered, 16 + 16 * 2 * TB * (SEQS - 1))
            rsqrt(SEQS - 1)
            pool.wait_ge(route_chain, RC * SEQS)
            scatter(SEQS - 1)

            for k in range(2):
                pool.wait_ge(ys_out[k], 16 * (BLOCKS // 2))
            for s in range(SEQS):
                k = s % 2
                pool.wait_ge(table_chain, TC)
                if s >= 2:
                    pool.wait_ge(summed, 2 * TB * (s - 1))
                for b in range(TB):
                    for c in range(2):
                        pool.indirect_dma_start(fetched[:, k, c, b], None, ys_dram,
                                                bass.IndirectOffsetOnAxis(ap=rows_out[:, s, c, b:b + 1], axis=0),
                                                ).then_inc(fetched_in[k], 16)
                if s >= 1:
                    pool.wait_ge(ln2_chain, LN * s)
                    pool.tensor_tensor(rstd[:], veps[:], minus_half[:], ALU.pow).then_inc(rstd2_done, 1)
            pool.wait_ge(ln2_chain, LN * SEQS)
            pool.tensor_tensor(rstd[:], veps[:], minus_half[:], ALU.pow).then_inc(rstd2_done, 1)

        @block.scalar
        def _(act):
            act.wait_ge(par_in, 16 * 11)
            act.activation(a_neg[:], a_neg[:], ACT.Exp).then_inc(prep_act, 1)

            def copy_in(name, s, dst, func=ACT.Copy, src=lambda bank: bank):
                b = BANK[name]
                act.wait_ge(filled[b], fills_before(name, s) + 1)
                act.activation(dst, src(ms[:, b]), func).then_inc(freed[b], 1)

            def front_at(n, s, q):
                t = s + 1
                first = isinstance(s, int) and s < 1
                if n == STEP["xt0"] + 1:
                    for k in range(KM):
                        copy_in(f"xt{k}", s, xT[:, k])
                for name, dts in (("in0", (0, 1)), ("in2", (2, 3))):
                    if n == STEP[name] + 1:
                        for d in dts:
                            act.wait_ge(filled[BANK[f"in{d}"]], fills_before(f"in{d}", s) + 1)
                            if d == 0 and not (isinstance(s, int) and s < 0):
                                act.wait_ge(du_done, t)
                            act.activation(xc[:, d], ms[:, BANK[f"in{d}"]], ACT.Identity, bias=cb[:, d:d + 1],
                                           scale=cw[:, d, TAPS - 1:TAPS]).then_inc(conv_first, 1)
                    if n == STEP[name] + 2:
                        for d in dts:
                            wait_copied(act, f"in{d}", s)
                            act.activation(xc[:, d], xc[:, d], ACT.Silu).then_inc(silu_done, 1)
                for name, tbs in (("z0", (0, 1)), ("z2", (2, 3))):
                    if n == STEP[name] + 1:
                        for b in tbs:
                            copy_in(f"z{b}", s, zs[:, q, b], ACT.Silu)
                if n == STEP["dt"] + 1:
                    copy_in("dt", s, dtr[:])
                    copy_in("b", s, b_sb[:], src=lambda bank: bank[0:N, :])
                if n == STEP["dt"] + 2:
                    wait_copied(act, "dt", s)
                    for d in range(DT):
                        act.activation(delta[:, q, d], dtr[:], ACT.Abs, bias=bdt[:, d:d + 1],
                                       scale=wdt[:, d:d + 1]).then_inc(sp_chain, 1)
                if n == STEP["c"] + 1:
                    copy_in("c", s, c_sb[:, q].rearrange("p b n -> p (b n)"),
                            src=lambda bank: bank[:, 0:TB * N])
                if n == STEP["dt"] + 3:
                    for d in range(DT):
                        act.activation(du[:, q, d], dtr[:], ACT.Relu, bias=bdt[:, d:d + 1],
                                       scale=wdt[:, d:d + 1]).then_inc(sp_chain, 1)
                    act.wait_ge(sp_chain, SPC * t + DT)
                    act.activation(delta[:, q], delta[:, q], ACT.Exp, scale=-1.0).then_inc(sp_chain, 1)
                if n == STEP["dt"] + 4:
                    act.wait_ge(sp_chain, SPC * t + 2 * DT + 1)
                    act.activation(delta[:, q], delta[:, q], ACT.Ln, bias=1.0).then_inc(sp_chain, 1)
                for b in range(TB):
                    if n == min(STEP[f"d{b}"] + 1, N):
                        copy_in(f"d{b}", s, y[:, q, b])

            def back_at(n, s, q):
                for name, tbs in (("g0", (0, 1)), ("g2", (2, 3))):
                    if n == STEP[name] + 1:
                        for b in tbs:
                            copy_in(f"g{b}", s, gT[:, b].rearrange("p k t -> p (k t)"))
                if n == STEP["rt0"] + 1:
                    for k in range(KM):
                        copy_in(f"rt{k}", s, xnT[:, k])
                if n == STEP["lg"] + 2:
                    wait_copied(act, "lg", s)
                    act.activation(prob[:], shifted[:], ACT.Exp).then_inc(exp_done, 1)

            def body(s, par, back, front):
                for n in range(N):
                    for half in range(2):
                        if half == 0 and n == 0:
                            act.wait_ge(delta_done, s + 1)
                        if n >= 1 or not isinstance(s, int) or s > 0:
                            act.wait_ge(scanned, HALVES * s + 2 * n + half - 1)
                        act.activation(dA[:, half, :, 1:T], delta[:, par, 2 * half:2 * half + 2, 1:T], ACT.Exp,
                                       scale=a_neg[:, n:n + 1]).then_inc(da_ready, 1)
                    if back:
                        back_at(n, s, 1 - par)
                    if front:
                        front_at(n, s, 1 - par)
                if front:
                    front_at(N, s, 1 - par)

            for n in range(N + 1):
                front_at(n, -1, 0)
            act.wait_ge(prep_dve, 3)
            sequences(act, body)
            for n in range(N):
                back_at(n, SEQS, (SEQS - 1) % 2)

            def copy_rows(j, k):
                act.wait_ge(xs_turned, j + 1)
                act.activation(xsT[:, k].rearrange("p c t -> p (c t)"), psum[:, 4 * k, 0:DM], ACT.Copy).then_inc(xs_copied, 1)

            def act_gate(j, k):
                act.wait_ge(gate_ready, j + 1)
                act.activation(gate_act[:, k], psum[:, 4 * k + 1], ACT.Silu).then_inc(gate_acted, 1)

            def copy_hidden(j, k):
                act.wait_ge(hid_turned, j + 1)
                act.activation(hidT[:, k].rearrange("p c t -> p (c t)"), psum[:, 4 * k + 3], ACT.Copy).then_inc(hid_copied, 1)

            def step(j, k, last=False):
                act_gate(j, k)
                if not (isinstance(j, int) and j == 0):
                    copy_hidden(j - 1, 1 - k)
                if not last:
                    copy_rows(j + 1, 1 - k)

            copy_rows(0, 0)
            for j in range(FIRST):
                step(j, j % 2)
            block_loop(act, step)
            step(BLOCKS - 1, (BLOCKS - 1) % 2, last=True)
            copy_hidden(BLOCKS - 1, (BLOCKS - 1) % 2)

        @block.vector
        def _(dve):
            dve.wait_ge(consts, 11)
            dve.wait_ge(par_in, 16 * 11)
            dve.wait_ge(prep_act, 1)
            dve.tensor_scalar(a_neg[:], a_neg[:], -1.0, None, ALU.mult).then_inc(prep_dve, 1)
            for h in range(2):
                dve.memset(dA[:, h, :, 0:1], 0.0).then_inc(prep_dve, 1)
            dve.tensor_copy(w_dtrep[:], w_x[:, :, 0:1].to_broadcast([P, DT, P])).then_inc(prep_dve, 1)
            for d in range(DT):
                dve.tensor_scalar(diag_d[:, d], ident[:], dp[:, d:d + 1], None, ALU.mult).then_inc(prep_dve, 1)
            dve.tensor_copy(base[:, TB:TB + 1], region0[:]).then_inc(prep_dve, 1)
            dve.wait_ge(bias_in, 16 * 3)
            dve.tensor_copy(bias_h[:, 0], bias_f[:, 0]).then_inc(bias_chain, 1)
            dve.wait_ge(bias_chain, 1)
            dve.tensor_tensor(bias_f[:, 1], bias_f[:, 0], bias_h[:, 0], ALU.subtract).then_inc(bias_chain, 1)
            dve.wait_ge(bias_chain, 2)
            dve.tensor_copy(bias_h[:, 1], bias_f[:, 1]).then_inc(bias_chain, 1)
            dve.wait_ge(bias_chain, 3)
            dve.tensor_tensor(bias_f[:, 0], bias_f[:, 1], bias_h[:, 1], ALU.subtract).then_inc(bias_chain, 1)
            dve.wait_ge(bias_chain, 4)
            dve.tensor_copy(bias_h[:, 2], bias_f[:, 0]).then_inc(bias_chain, 1)

            def front_at(n, s, q):
                for name, dts in (("in0", (0, 1)), ("in2", (2, 3))):
                    if n == STEP[name] + 1:
                        for d in dts:
                            dve.wait_ge(conv_first, DT * (s + 1) + d + 1)
                        at = (TAPS - 2) * (DT * (s + 1) + dts[0])
                        for j in range(1, TAPS):
                            for d in dts:
                                if j > 1:
                                    dve.wait_ge(conv_chain, at + 2 * (j - 2) + (d - dts[0]) + 1)
                                bank = ms[:, BANK[f"in{d}"]]
                                ins = dve.scalar_tensor_tensor(xc[:, d, j:T], bank[:, 0:T - j], cw[:, d, TAPS - 1 - j:TAPS - j],
                                                               xc[:, d, j:T], ALU.mult, ALU.add)
                                ins.then_inc(conv_chain if j < TAPS - 1 else freed[BANK[f"in{d}"]], 1)

            def moments(chain, at):
                dve.wait_ge(chain, at + TB)
                dve.tensor_tensor(mean2[:], stats[:, :, 1], stats[:, :, 4], ALU.add).then_inc(chain, 1)
                dve.tensor_tensor(apart[:], stats[:, :, 1], stats[:, :, 4], ALU.subtract).then_inc(chain, 1)
                dve.tensor_tensor(squares[:], stats[:, :, 2], stats[:, :, 5], ALU.add).then_inc(chain, 1)
                dve.wait_ge(chain, at + TB + 3)
                dve.tensor_tensor(apart[:], apart[:], apart[:], ALU.mult).then_inc(chain, 1)
                dve.tensor_scalar(mean[:], mean2[:], 0.5, None, ALU.mult).then_inc(chain, 1)
                dve.tensor_scalar(squares[:], squares[:], 1.0 / DM, EPS, ALU.mult, ALU.add).then_inc(chain, 1)
                dve.wait_ge(chain, at + TB + 6)
                dve.scalar_tensor_tensor(veps[:], apart[:], 0.25, squares[:], ALU.mult, ALU.add).then_inc(chain, 1)

            def back_at(n, s):
                r = s - 1
                if n == STEP["o0"] + 1:
                    dve.wait_ge(x_res_in, 16 * s)
                    for h in range(2):
                        b = BANK[f"o{h}"]
                        dve.wait_ge(filled[b], fills_before(f"o{h}", s) + 1)
                        dve.tensor_tensor(res[:, 2 * h:2 * h + 2].rearrange("p b m -> p (b m)"), ms[:, b],
                                          x_res[:, 2 * h:2 * h + 2].rearrange("p b m -> p (b m)"), ALU.add).then_inc(freed[b], 1)
                    for b in range(TB):
                        dve.wait_ge(freed[BANK[f"o{b // 2}"]], fills_before(f"o{b // 2}", s) + 1)
                        dve.bn_stats(stats[:, b], res[:, b]).then_inc(ln_chain, 1)
                    moments(ln_chain, LN * r)
                if n == STEP["o0"] + 2:
                    dve.wait_ge(rstd_done, r + 1)
                    for b in range(TB):
                        dve.tensor_scalar(xn[:, b], res[:, b], mean[:, b:b + 1], rstd[:, b:b + 1],
                                          ALU.subtract, ALU.mult).then_inc(xn_done, 1)

            def route_at(n, s):
                r = s - 1
                at = RC * r
                wide = [P, TB, E]
                logits = ms[:, BANK["lg"], 0:TB * E].rearrange("p (b e) -> p b e", e=E)
                first_of = falling[:].to_broadcast(wide)
                if n == STEP["lg"] + 1:
                    dve.wait_ge(filled[BANK["lg"]], fills_before("lg", s) + 1)
                    dve.tensor_reduce(top[:, 0, :, 0], logits, X, ALU.max).then_inc(route_chain, 1)
                    dve.wait_ge(route_chain, at + 1)
                    dve.tensor_tensor(shifted[:], logits, top[:, 0].to_broadcast(wide), ALU.subtract).then_inc(freed[BANK["lg"]], 1)
                if n == STEP["lg"] + 2:
                    at = at + RC1
                    dve.wait_ge(exp_done, r + 1)
                    steps = [
                        lambda: dve.tensor_reduce(top[:, 1, :, 0], prob[:], X, ALU.add),
                        lambda: dve.reciprocal(top[:, 2], top[:, 1]),
                        lambda: dve.tensor_tensor(prob[:], prob[:], top[:, 2].to_broadcast(wide), ALU.mult),
                    ]
                    for m, make in enumerate(steps):
                        if m:
                            dve.wait_ge(route_chain, at + m)
                        make().then_inc(route_chain, 1)
                    at = at + 3
                    for c, left in ((0, prob), (1, equal)):
                        dve.wait_ge(route_chain, at + 6 * c)
                        dve.tensor_reduce(top[:, 3 + c, :, 0], left[:], X, ALU.max).then_inc(route_chain, 1)
                        dve.wait_ge(route_chain, at + 6 * c + 1)
                        dve.tensor_tensor(both[:], left[:], top[:, 3 + c].to_broadcast(wide), ALU.is_equal).then_inc(route_chain, 1)
                        dve.wait_ge(route_chain, at + 6 * c + 2)
                        dve.tensor_tensor(both[:], both[:], first_of, ALU.mult).then_inc(route_chain, 1)
                        dve.wait_ge(route_chain, at + 6 * c + 3)
                        dve.tensor_reduce(top[:, 5, :, 0], both[:], X, ALU.max).then_inc(route_chain, 1)
                        dve.wait_ge(route_chain, at + 6 * c + 4)
                        dve.tensor_tensor(pick[:, c], first_of, top[:, 5].to_broadcast(wide), ALU.is_equal).then_inc(route_chain, 1)
                        dve.wait_ge(route_chain, at + 6 * c + 5)
                        if c == 0:
                            dve.scalar_tensor_tensor(equal[:], pick[:, 0], -2.0, prob[:], ALU.mult, ALU.add).then_inc(route_chain, 1)
                        else:
                            dve.tensor_tensor(both[:], pick[:, 0], pick[:, 1], ALU.add).then_inc(route_chain, 1)
                if n == STEP["pf"] + 1:
                    at = at + RC1 + RC2
                    bank = ms[:, BANK["pf"]]
                    ahead = bank[:, 0:TB * E].rearrange("p (b e) -> p b e", e=E)
                    total = bank[:, TB * E:2 * TB * E].rearrange("p (b e) -> p b e", e=E)
                    dve.wait_ge(filled[BANK["pf"]], fills_before("pf", s) + 1)
                    dve.tensor_copy(base[:, 0], base[:, TB]).then_inc(route_chain, 1)
                    for b in range(TB):
                        dve.wait_ge(route_chain, at + b + 1)
                        dve.tensor_tensor(base[:, b + 1], base[:, b], total[:, b], ALU.add).then_inc(route_chain, 1)
                    dve.wait_ge(route_chain, at + TB + 1)
                    dve.tensor_tensor(row_of[:], ahead, base[:, 0:TB], ALU.add).then_inc(freed[BANK["pf"]], 1)
                    wait_copied(dve, "pf", s)
                    dve.tensor_tensor(equal[:], row_of[:], pick[:, 0], ALU.mult).then_inc(route_chain, 1)
                    dve.tensor_tensor(shifted[:], row_of[:], pick[:, 1], ALU.mult).then_inc(route_chain, 1)
                    dve.tensor_tensor(top[:, 6], top[:, 3], top[:, 4], ALU.add).then_inc(route_chain, 1)
                    at = at + TB + 4
                    dve.wait_ge(route_chain, at)
                    dve.tensor_reduce(rows_f[:, 0], equal[:], X, ALU.add).then_inc(route_chain, 1)
                    dve.tensor_reduce(rows_f[:, 1], shifted[:], X, ALU.add).then_inc(route_chain, 1)
                    dve.tensor_scalar(top[:, 6], top[:, 6], 1e-9, None, ALU.add).then_inc(route_chain, 1)
                    dve.wait_ge(route_chain, at + 3)
                    dve.tensor_copy(route_rows, rows_f[:]).then_inc(route_chain, 1)
                    dve.reciprocal(top[:, 7], top[:, 6]).then_inc(route_chain, 1)
                    dve.wait_ge(route_chain, at + 5)
                    dve.tensor_tensor(route[:, 2], top[:, 3, :, 0], top[:, 7, :, 0], ALU.mult).then_inc(route_chain, 1)
                    dve.tensor_tensor(route[:, 3], top[:, 4, :, 0], top[:, 7, :, 0], ALU.mult).then_inc(route_chain, 1)

            def add_state(s, n, b, par):
                dve.wait_ge(ht_ready, PIECES * s + TB * n + b + 1)
                if n > 0:
                    dve.wait_ge(y_added, PIECES * s + TB * (n - 1) + b + 1)
                dve.scalar_tensor_tensor(y[:, par, b], hT[:, b % 2], c_sb[:, par, b, n:n + 1], y[:, par, b],
                                         ALU.mult, ALU.add).then_inc(y_added, 1)

            def body(s, par, back, front):
                for n in range(N):
                    for half in range(2):
                        dve.wait_ge(da_ready, HALVES * s + 2 * n + half + 1)
                        if half == 0:
                            dve.wait_ge(input_ready, N * s + n + 1)
                        v = state[:, n % RING, 2 * half:2 * half + 2].rearrange("p d t -> p (d t)")
                        dve.tensor_tensor_scan(v, dA[:, half].rearrange("p d t -> p (d t)"), v, 0.0,
                                               ALU.mult, ALU.add).then_inc(scanned, 1)
                        if n > 0:
                            for b in (2 * half, 2 * half + 1):
                                add_state(s, n - 1, b, par)
                    if back:
                        back_at(n, s)
                        route_at(n, s)
                    if front:
                        front_at(n, s, 1 - par)
                for b in range(TB):
                    add_state(s, N - 1, b, par)

            for n in range(N + 1):
                front_at(n, -1, 0)
            sequences(dve, body)
            for n in range(N):
                back_at(n, SEQS)
                route_at(n, SEQS)

            count = [0]

            def chain(ins):
                count[0] += 1
                ins.then_inc(table_chain, 1)
                dve.wait_ge(table_chain, count[0])

            grid = [P, BLOCKS, E]
            used, n_blocks, end, start, offset, expert = (blocks[:, m] for m in range(6))
            dve.wait_ge(route_chain, RC * SEQS)
            chain(dve.tensor_copy(ends_i[:], base[:, TB:TB + 1]))
            chain(dve.tensor_tensor(used, base[:, TB:TB + 1], region0[:], ALU.subtract))
            chain(dve.tensor_scalar(used_i[:], used, float(P - 1), None, ALU.add))
            chain(dve.tensor_scalar(used_i[:], used_i[:], P.bit_length() - 1, None, ALU.arith_shift_right))
            chain(dve.tensor_copy(n_blocks, used_i[:]))
            chain(dve.tensor_tensor_scan(end[:, 0], ones[:, 0:E], n_blocks[:, 0], 0.0, ALU.mult, ALU.add))
            chain(dve.tensor_tensor(start, end, n_blocks, ALU.subtract))
            chain(dve.scalar_tensor_tensor(offset, start, -float(P), region0[:], ALU.mult, ALU.add))
            numbers = number[:].to_broadcast(grid)
            chain(dve.tensor_tensor(inside[:, 0], numbers, start.to_broadcast(grid), ALU.is_ge))
            chain(dve.tensor_tensor(inside[:, 1], numbers, end.to_broadcast(grid), ALU.is_lt))
            chain(dve.tensor_tensor(inside[:, 0], inside[:, 0], inside[:, 1], ALU.mult))
            chain(dve.tensor_reduce(sums[:, 0], inside[:, 0], X, ALU.add))
            chain(dve.tensor_tensor(inside[:, 1], inside[:, 0], expert.to_broadcast(grid), ALU.mult))
            chain(dve.tensor_reduce(sums[:, 1], inside[:, 1], X, ALU.add))
            chain(dve.tensor_tensor(inside[:, 1], inside[:, 0], offset.to_broadcast(grid), ALU.mult))
            chain(dve.tensor_reduce(sums[:, 2], inside[:, 1], X, ALU.add))
            chain(dve.tensor_scalar(sums[:, 3], sums[:, 0], -float(DUMP - 2 * TOK), float(DUMP - 2 * TOK), ALU.mult, ALU.add))
            chain(dve.tensor_tensor(sums[:, 3], sums[:, 3], sums[:, 2], ALU.add))
            chain(dve.scalar_tensor_tensor(table[:, 0], number[:, :, 0], float(P), sums[:, 3], ALU.mult, ALU.add))
            chain(dve.tensor_copy(table[:, 1], sums[:, 1]))
            chain(dve.tensor_scalar(table[:, 2], number[:, :, 0], float(P), None, ALU.mult))
            shape = [P, SEQS * 2 * TB, E]
            rows_in = routes[:, :, 0:2].bitcast(U32)
            in_region, weighed = (inside[:, m, 0:shape[1]] for m in range(2))
            flat = rows_f2.rearrange("p s c b -> p (s c b)")
            chain(dve.tensor_copy(end[:, :, 1:E], offset[:, :, 0:E - 1]))
            chain(dve.memset(end[:, :, 0:1], 0.0))
            chain(dve.tensor_tensor(end, offset, end, ALU.subtract))
            dve.wait_ge(route_in, 16)
            chain(dve.tensor_copy(rows_f2, rows_in))
            chain(dve.tensor_tensor(in_region, xc[:, 2, 0:shape[1]].rearrange("p (r o) -> p r o", o=1).to_broadcast(shape), region0[:].to_broadcast(shape), ALU.is_ge))
            chain(dve.tensor_tensor(weighed, in_region, end.to_broadcast(shape), ALU.mult))
            chain(dve.tensor_reduce(sums[:, 0, 0:shape[1]], weighed, X, ALU.add))
            chain(dve.tensor_tensor(rows_out.rearrange("p s c b -> p (s c b)"), flat, sums[:, 0, 0:shape[1]], ALU.subtract))
            assert count[0] == TC

            def gate_up(j, k):
                dve.wait_ge(up_ready, j + 1)
                dve.wait_ge(gate_acted, j + 1)
                dve.tensor_tensor(hid[:, k], gate_act[:, k], psum[:, 4 * k + 2], ALU.mult).then_inc(hid_ready, 1)

            def copy_result(j, k):
                dve.wait_ge(down_ready, j + 1)
                if not (isinstance(j, int) and j < 2):
                    dve.wait_ge(ys_out[k], 16 * (j // 2) if isinstance(j, int) else 8 * (j - k))
                dve.tensor_copy(ys[:, k], psum[:, 4 * k, DM:2 * DM]).then_inc(ys_copied, 1)

            def step(j, k):
                gate_up(j, k)
                if not (isinstance(j, int) and j == 0):
                    copy_result(j - 1, 1 - k)

            for j in range(FIRST):
                step(j, j % 2)
            block_loop(dve, step)
            step(BLOCKS - 1, (BLOCKS - 1) % 2)
            copy_result(BLOCKS - 1, (BLOCKS - 1) % 2)

            for s in range(SEQS):
                k = s % 2
                at = LN * s
                dve.wait_ge(fetched_in[k], 16 * 2 * TB * (s // 2 + 1))
                dve.wait_ge(resid_in[k], 16 * (s // 2 + 1))
                for c in range(2):
                    for b in range(TB):
                        if c:
                            dve.wait_ge(summed, 2 * TB * s + b + 1)
                        dve.scalar_tensor_tensor(resid[:, k, b], fetched[:, k, c, b], routes[:, s, 2 + c, b:b + 1], resid[:, k, b],
                                                 ALU.mult, ALU.add).then_inc(summed, 1)
                for b in range(TB):
                    dve.wait_ge(summed, 2 * TB * s + TB + b + 1)
                    dve.bn_stats(stats[:, b], resid[:, k, b]).then_inc(ln2_chain, 1)
                moments(ln2_chain, at)
                dve.wait_ge(rstd2_done, s + 1)
                if s >= 2:
                    dve.wait_ge(out_stored[k], 16 * (s // 2))
                for b in range(TB):
                    dve.tensor_scalar(outs[:, k, b], resid[:, k, b], mean[:, b:b + 1], rstd[:, b:b + 1],
                                      ALU.subtract, ALU.mult).then_inc(normed, 1)

        @block.tensor
        def _(pe):
            pe.wait_ge(consts, 11)
            pe.wait_ge(par_in, 16 * 11)
            pe.wait_ge(prep_dve, 4 + DT)

            def fill(name, s):
                b, before_ = BANK[name], fills_before(name, s)
                if not (isinstance(before_, int) and before_ == 0):
                    pe.wait_ge(freed[b], before_)
                return ms[:, b]

            def front_at(n, s, q):
                t = s + 1
                if n == STEP["xt0"]:
                    pe.wait_ge(x_in, 16 * (t + 1))
                    for k in range(KM):
                        bank = fill(f"xt{k}", s)
                        for b in range(TB):
                            ins = pe.transpose(bank[:, b * P:(b + 1) * P], x_sb[:, b, k * P:(k + 1) * P], ident[:])
                        ins.then_inc(filled[BANK[f"xt{k}"]], 1)
                for d in range(DT):
                    if n == STEP[f"in{d}"]:
                        for k in range(KM):
                            wait_copied(pe, f"xt{k}", s)
                        bank = fill(f"in{d}", s)
                        for k in range(KM):
                            ins = pe.matmul(bank, w_in[:, k, d * P:(d + 1) * P], xT[:, k], start=k == 0, stop=k == KM - 1)
                        ins.then_inc(filled[BANK[f"in{d}"]], 1)
                for b in range(TB):
                    if n == STEP[f"z{b}"]:
                        bank = fill(f"z{b}", s)
                        for k in range(KM):
                            ins = pe.matmul(bank, xT[:, k, b * P:(b + 1) * P], w_in[:, k, DI:2 * DI], start=k == 0, stop=k == KM - 1)
                        ins.then_inc(filled[BANK[f"z{b}"]], 1)
                if n == STEP["dt"]:
                    pe.wait_ge(silu_done, DT * (t + 1))
                    bank = fill("dt", s)
                    for k in range(DT):
                        ins = pe.matmul(bank, w_dtrep[:, k], xc[:, k], start=k == 0, stop=k == DT - 1)
                    ins.then_inc(filled[BANK["dt"]], 1)
                    bank = fill("b", s)
                    for k in range(DT):
                        ins = pe.matmul(bank[0:N, :], w_x[:, k, 1:1 + N], xc[:, k], start=k == 0, stop=k == DT - 1)
                    ins.then_inc(filled[BANK["b"]], 1)
                if n == STEP["c"]:
                    bank = fill("c", s)
                    for b in range(TB):
                        for k in range(DT):
                            ins = pe.matmul(bank[:, b * N:(b + 1) * N], xc[:, k, b * P:(b + 1) * P], w_x[:, k, 1 + N:1 + 2 * N],
                                            start=k == 0, stop=k == DT - 1)
                    ins.then_inc(filled[BANK["c"]], 1)
                for b in range(TB):
                    if n == STEP[f"d{b}"]:
                        bank = fill(f"d{b}", s)
                        for k in range(DT):
                            ins = pe.matmul(bank[:, k * P:(k + 1) * P], xc[:, k, b * P:(b + 1) * P], diag_d[:, k], start=True, stop=True)
                        ins.then_inc(filled[BANK[f"d{b}"]], 1)

            def back_at(n, s, q):
                for b in range(TB):
                    if n == STEP[f"g{b}"]:
                        pe.wait_ge(gated, s)
                        bank = fill(f"g{b}", s)
                        for k in range(DT):
                            ins = pe.transpose(bank[:, k * P:(k + 1) * P], y[:, q, b, k * P:(k + 1) * P], ident[:])
                        ins.then_inc(filled[BANK[f"g{b}"]], 1)
                for h in range(2):
                    if n == STEP[f"o{h}"]:
                        for b in range(2 * h, 2 * h + 2):
                            wait_copied(pe, f"g{b}", s)
                        bank = fill(f"o{h}", s)
                        for b in range(2 * h, 2 * h + 2):
                            for k in range(DT):
                                ins = pe.matmul(bank[:, (b % 2) * DM:(b % 2 + 1) * DM], gT[:, b, k], w_out[:, k],
                                                start=k == 0, stop=k == DT - 1)
                        ins.then_inc(filled[BANK[f"o{h}"]], 1)
                if n == STEP["rt0"]:
                    pe.wait_ge(xn_done, TB * s)
                    for k in range(KM):
                        bank = fill(f"rt{k}", s)
                        for b in range(TB):
                            ins = pe.transpose(bank[:, b * P:(b + 1) * P], xn[:, b, k * P:(k + 1) * P], ident[:])
                        ins.then_inc(filled[BANK[f"rt{k}"]], 1)
                if n == STEP["lg"]:
                    bank = fill("lg", s)
                    for k in range(KM):
                        wait_copied(pe, f"rt{k}", s)
                    for b in range(TB):
                        for k in range(KM):
                            ins = pe.matmul(bank[:, b * E:(b + 1) * E], xnT[:, k, b * P:(b + 1) * P], w_rt[:, k],
                                            start=k == 0, stop=k == KM - 1)
                    ins.then_inc(filled[BANK["lg"]], 1)
                if n == STEP["pf"]:
                    pe.wait_ge(route_chain, RC * (s - 1) + RC1 + RC2)
                    bank = fill("pf", s)
                    picks = both[:].rearrange("p b e -> p (b e)")
                    pe.matmul(bank[:, 0:TB * E], before[:], picks, start=True, stop=True)
                    ins = pe.matmul(bank[:, TB * E:2 * TB * E], ones[:], picks, start=True, stop=True)
                    ins.then_inc(filled[BANK["pf"]], 1)

            def body(s, par, back, front):
                for n in range(N):
                    pe.wait_ge(scanned, HALVES * s + 2 * n + 2)
                    for b in range(TB):
                        at = TB * n + b
                        if at >= 2 or not isinstance(s, int) or s > 0:
                            pe.wait_ge(y_added, PIECES * s + at - 1)
                        for d in range(DT):
                            ins = pe.transpose(hT[:, b % 2, d * P:(d + 1) * P], state[:, n % RING, d, b * P:(b + 1) * P], ident[:])
                        ins.then_inc(ht_ready, 1)
                    if back:
                        back_at(n, s, 1 - par)
                    if front:
                        front_at(n, s, 1 - par)

            for n in range(N):
                front_at(n, -1, 0)
            sequences(pe, body)
            for n in range(N):
                back_at(n, SEQS, (SEQS - 1) % 2)

            pe.wait_ge(table_chain, TC)
            pe.wait_ge(w_loaded, 16 * 4)

            def expert_of(j):
                return pe.value_load(table[0:1, 1, bass.ds(j, 1)], min_val=0, max_val=E - 1)

            def turn_rows(j, k):
                pe.wait_ge(xs_in[k], 16 * (j // 2 + 1) if isinstance(j, int) else 8 * (j - k) + 16)
                if not (isinstance(j, int) and j < 4):
                    pe.wait_ge(ys_copied, j - 3)
                for c in range(KM):
                    ins = pe.transpose(psum[:, 4 * k, c * P:(c + 1) * P], xs[:, k, c * P:(c + 1) * P], ident[:])
                ins.then_inc(xs_turned, 1)

            def project(j, k, e, bank, w, bias, signal):
                for c in range(KM):
                    pe.matmul(psum[:, bank], xsT[:, k, c], w[:, bass.ds(e, 1), c].rearrange("p o f -> p (o f)"), start=c == 0, stop=False)
                pe.matmul(psum[:, bank], bf_ones[:], bias[:, bass.ds(e, 1)].rearrange("p o f -> p (o f)"),
                          start=False, stop=True).then_inc(signal, 1)

            def gate(j, k, e):
                pe.wait_ge(xs_copied, j + 1)
                if not (isinstance(j, int) and j < 2):
                    pe.wait_ge(gate_acted, j - 1)
                project(j, k, e, 4 * k + 1, w_gate, g_bias, gate_ready)

            def up(j, k, e):
                if not (isinstance(j, int) and j < 2):
                    pe.wait_ge(hid_ready, j - 1)
                project(j, k, e, 4 * k + 2, w_up, u_bias, up_ready)

            def turn_hidden(j, k):
                pe.wait_ge(hid_ready, j + 1)
                if not (isinstance(j, int) and j < 2):
                    pe.wait_ge(hid_copied, j - 1)
                for c in range(FB):
                    ins = pe.transpose(psum[:, 4 * k + 3, c * P:(c + 1) * P], hid[:, k, c * P:(c + 1) * P], ident[:])
                ins.then_inc(hid_turned, 1)

            def down(j, k, e):
                pe.wait_ge(hid_copied, j + 1)
                if isinstance(j, int) and j + 2 >= BLOCKS:
                    pe.wait_ge(xs_copied, BLOCKS)
                else:
                    pe.wait_ge(xs_copied, j + 3)
                if not (isinstance(j, int) and j < 2):
                    pe.wait_ge(ys_copied, j - 1)
                result = psum[:, 4 * k, DM:2 * DM]
                for c in range(FB):
                    pe.matmul(result, hidT[:, k, c], w_down[:, bass.ds(e, 1), c].rearrange("p o m -> p (o m)"), start=c == 0, stop=False)
                pe.matmul(result, bf_ones[:], d_bias[:, bass.ds(e, 1)].rearrange("p o m -> p (o m)"),
                          start=False, stop=True).then_inc(down_ready, 1)

            def step(j, k, last=False):
                e = expert_of(j)
                gate(j, k, e)
                more = not (isinstance(j, int) and j == 0)
                if more:
                    turn_hidden(j - 1, 1 - k)
                if not last:
                    turn_rows(j + 1, 1 - k)
                up(j, k, e)
                if more:
                    down(j - 1, 1 - k, expert_of(j - 1))

            turn_rows(0, 0)
            for j in range(FIRST):
                step(j, j % 2)
            block_loop(pe, step)
            step(BLOCKS - 1, (BLOCKS - 1) % 2, last=True)
            turn_hidden(BLOCKS - 1, (BLOCKS - 1) % 2)
            down(BLOCKS - 1, (BLOCKS - 1) % 2, expert_of(BLOCKS - 1))


_INS = ['L0_attn_x', 'L0_attn_W_in', 'L0_attn_conv_w', 'L0_attn_conv_b', 'L0_attn_W_xproj', 'L0_attn_W_dt',
        'L0_attn_b_dt', 'L0_attn_A_log', 'L0_attn_Dp', 'L0_attn_W_out', 'L0_ffn_router_w', 'L0_ffn_gate_w',
        'L0_ffn_gate_b', 'L0_ffn_up_w', 'L0_ffn_up_b', 'L0_ffn_down_w', 'L0_ffn_down_b']
_OUTS = [((SEQS, T, DM), 'float32')]


def kernel(**inputs):
    import numpy as _np
    import concourse.bacc as _bacc
    from concourse import mybir as _mybir
    from concourse.bass_utils import run_bass_kernel_spmd as _run

    nc = _bacc.Bacc("TRN2", target_bir_lowering=False, num_devices=1)
    arrays, args = {}, []
    for name in _INS:
        a = _np.ascontiguousarray(inputs[name])
        arrays[f"in_{name}_dram"] = a
        args.append(nc.dram_tensor(f"in_{name}_dram", a.shape, _mybir.dt.from_np(a.dtype), kind="ExternalInput").ap())
    for i, (shape, dtype) in enumerate(_OUTS):
        dt = _mybir.dt.from_np(_np.dtype(dtype))
        args.append(nc.dram_tensor(f"out_{i}_dram", shape, dt, kind="ExternalOutput").ap())
    mamba_moe_program(nc, *args)
    r = _run(nc, [arrays], core_ids=[0])
    return r.results[0]["out_0_dram"]
```

```python
from contextlib import ExitStack

import concourse.bass as bass
from concourse import mybir

ALU = mybir.AluOpType
ACT = mybir.ActivationFunctionType
F32 = mybir.dt.float32
BF16 = mybir.dt.bfloat16
I32 = mybir.dt.int32
U32 = mybir.dt.uint32
X = mybir.AxisListType.X

P = 128
SEQS, T, DM = 8, 512, 256
DI, N, TAPS = 512, 16, 4
E, FF = 8, 512
TB = T // P
DT = DI // P
KM = DM // P
FB = FF // P
TILES = SEQS * TB
TOK = SEQS * T
RING = 4
BG = 4
REGION = TOK + P
DUMP = E * REGION
BLOCKS = 2 * TOK // P + E - 1
BLOCKS += BLOCKS % 2
SPARE = BLOCKS - 2 * TOK // P
EPS = 1e-5
NB = E * (2 * FF + DM)

USES = [
    ("xt0", "front", 0, 0), ("xt1", "front", 1, 0), ("in0", "front", 0, 1), ("z0", "front", 1, 1),
    ("in1", "front", 0, 2), ("g0", "back", 1, 2), ("in2", "front", 0, 3), ("g1", "back", 1, 3),
    ("in3", "front", 0, 4), ("g2", "back", 1, 4), ("g3", "back", 1, 5), ("o0", "back", 0, 5),
    ("o1", "back", 1, 6), ("bc", "front", 0, 7), ("z1", "front", 0, 8), ("z2", "front", 1, 8),
    ("c", "front", 0, 9), ("d0", "front", 1, 9), ("rt0", "back", 0, 10), ("rt1", "back", 1, 10),
    ("lg", "back", 0, 11), ("z3", "front", 1, 12), ("d1", "front", 0, 13), ("d2", "front", 1, 13),
    ("pf", "back", 0, 14), ("d3", "front", 1, 14),
]
BANK = {name: bank for name, _, bank, _ in USES}
STEP = {name: step for name, _, _, step in USES}
PER = {(kind, b): sum(k == kind and bank == b for _, k, bank, _ in USES) for kind in ("front", "back") for b in (0, 1)}


def fills_before(name, s):
    b = BANK[name]
    at = [u[0] for u in USES].index(name)
    peeled = isinstance(s, int)
    kinds = [k for k, there in (("back", not peeled or s >= 1), ("front", not peeled or s <= SEQS - 2)) if there]
    here = sum(k in kinds and bank == b for _, k, bank, _ in USES[:at])
    if peeled:
        return PER["front", b] * min(s + 1, SEQS) + PER["back", b] * max(s - 1, 0) + here
    return (PER["front", b] + PER["back", b]) * s + (PER["front", b] - PER["back", b] + here)


def mamba_moe_program(nc, x, W_in, conv_w, conv_b, W_xproj, W_dt, b_dt, A_log, Dp, W_out,
                      router_w, gate_w, gate_b, up_w, up_b, down_w, down_b, out):
    x_rows = x.rearrange("s (b p) m -> s p b m", p=P)
    out_rows = out.rearrange("s (b p) m -> s p b m", p=P)
    xn_dram = nc.dram_tensor("xn_scratch", (SEQS, P, TB, DM), F32).ap()
    b_dram = nc.dram_tensor("b_scratch", (2, 1 + N, T), F32).ap()
    xs_dram = nc.dram_tensor("expert_in", (DUMP + SPARE * P, DM), F32).ap()
    ys_dram = nc.dram_tensor("expert_out", (BLOCKS * P, DM), F32).ap()
    route_dram = nc.dram_tensor("route_scratch", (SEQS, P, 4 * TB), F32).ap()
    bias_dram = nc.dram_tensor("bias_scratch", (3, NB), BF16).ap()

    with ExitStack() as ctx:
        def sb(name, shape, dt=F32):
            return ctx.enter_context(nc.sbuf_tensor(name, shape, dt))

        def ps(name, shape, dt=F32):
            return ctx.enter_context(nc.psum_tensor(name, shape, dt))

        def sem(name):
            return ctx.enter_context(nc.semaphore(name))

        ident = sb("ident", [P, P])
        before = sb("before", [P, P])
        ones = sb("ones", [P, P])
        w_in = sb("w_in", [P, KM, 2 * DI])
        w_out = sb("w_out", [P, DT, DM])
        w_x = sb("w_x", [P, DT, 2 * N + 1])
        w_rt = sb("w_rt", [P, KM, E])
        diag_d = sb("diag_d", [P, DT, P])
        cw = sb("cw", [P, DT, TAPS])
        cb = sb("cb", [P, DT])
        wdt = sb("wdt", [P, DT])
        bdt = sb("bdt", [P, DT])
        dp = sb("dp", [P, DT])
        a_neg = sb("a_neg", [P, N])
        minus_half = sb("minus_half", [P, TB])
        x_sb = sb("x_sb", [P, TB, DM])
        x_res = sb("x_res", [P, TB, DM])
        xT = sb("xT", [P, KM, T])
        xc = sb("xc", [P, DT, T])
        dtr = sb("dtr", [P, T])
        big = sb("big", [P, 3 * E * KM * FF])
        per = RING * DT * T
        state = big[:, 0:per].rearrange("p (r d t) -> p r d t", r=RING, d=DT)
        b_bc = big[:, per:2 * per].rearrange("p (n t) -> p n t", n=N)
        delta = big[:, 2 * per:5 * per // 2].rearrange("p (q d t) -> p q d t", q=2, d=DT)
        du = big[:, 5 * per // 2:3 * per].rearrange("p (q d t) -> p q d t", q=2, d=DT)
        mid = sb("mid", [P, 4 * TB * DI])
        zs = mid[:, 0:2 * TB * DI].rearrange("p (q b n) -> p q b n", q=2, b=TB)
        y = mid[:, 2 * TB * DI:].rearrange("p (q b n) -> p q b n", q=2, b=TB)
        c_sb = sb("c_sb", [P, 2, TB, N])
        bc_sb = sb("bc_sb", [P, T])
        gT = sb("gT", [P, TB, DT, P])
        res = sb("res", [P, TB, DM])
        xn = sb("xn", [P, TB, DM])
        xnT = sb("xnT", [P, KM, T])
        stats = sb("stats", [P, TB, 6])
        mean2 = sb("mean2", [P, TB])
        mean = sb("mean", [P, TB])
        apart = sb("apart", [P, TB])
        squares = sb("squares", [P, TB])
        veps = sb("veps", [P, TB])
        rstd = sb("rstd", [P, TB])
        falling = sb("falling", [P, 1, E])
        region0 = sb("region0", [P, 1, E])
        shifted = sb("shifted", [P, TB, E])
        prob = sb("prob", [P, TB, E])
        equal = sb("equal", [P, TB, E])
        pick = sb("pick", [P, 2, TB, E])
        both = sb("both", [P, TB, E])
        base = sb("base", [P, TB + 1, E])
        row_of = sb("row_of", [P, TB, E])
        top = sb("top", [P, 8, TB, 1])
        rows_f = sb("rows_f", [P, 2, TB])
        route = sb("route", [P, 4, TB])
        route_rows = route[:, 0:2].bitcast(U32)
        zeros = sb("zeros", [P, 1, DM])
        bias_f = sb("bias_f", [NB // P, 2, P])
        bias_h = sb("bias_h", [NB // P, 3, P], BF16)
        blocks = sb("blocks", [P, 6, 1, E])
        used_i = sb("used_i", [P, 1, E], I32)
        ends_i = sb("ends_i", [P, 1, E], I32)
        number = sb("number", [P, BLOCKS, 1])
        inside = sb("inside", [P, 2, BLOCKS, E])
        sums = sb("sums", [P, 4, BLOCKS])
        table = sb("table", [P, 3, BLOCKS], I32)

        w_gate = big[:, 0:E * KM * FF].rearrange("p (e k f) -> p e k f", e=E, k=KM)
        w_up = big[:, E * KM * FF:2 * E * KM * FF].rearrange("p (e k f) -> p e k f", e=E, k=KM)
        w_down = big[:, 2 * E * KM * FF:].rearrange("p (e k m) -> p e k m", e=E, k=FB)
        bias_w = mid[0:3, 0:NB // 2].bitcast(BF16)
        g_bias = bias_w[:, 0:E * FF].rearrange("p (e f) -> p e f", e=E)
        u_bias = bias_w[:, E * FF:2 * E * FF].rearrange("p (e f) -> p e f", e=E)
        d_bias = bias_w[:, 2 * E * FF:].rearrange("p (e m) -> p e m", e=E)
        free = NB // 2
        xs = mid[:, free:free + 2 * DM].rearrange("p (k m) -> p k m", k=2)
        xsT = mid[:, free + 512:free + 1024].rearrange("p (k c t) -> p k c t", k=2, c=KM)
        gate_act = mid[:, free + 1024:free + 2048].rearrange("p (k f) -> p k f", k=2)
        hid = mid[:, free + 2048:free + 3072].rearrange("p (k f) -> p k f", k=2)
        hidT = gT[:, 0:2]
        ys = xc[:, 0].rearrange("p (k m) -> p k m", k=2)
        routes = xc[:, 1, 0:SEQS * 4 * TB].rearrange("p (s c b) -> p s c b", s=SEQS, c=4)
        routes_flat = xc[:, 1, 0:SEQS * 4 * TB].rearrange("p (s c) -> p s c", s=SEQS)
        rows_f2 = xc[:, 2, 0:SEQS * 2 * TB].rearrange("p (s c b) -> p s c b", s=SEQS, c=2)
        rows_out = xc[:, 3, 0:SEQS * 2 * TB].bitcast(U32).rearrange("p (s c b) -> p s c b", s=SEQS, c=2)
        outs = mid[:, 0:2 * TB * DM].rearrange("p (k b m) -> p k b m", k=2, b=TB)
        fetched = mid[:, 2 * TB * DM:6 * TB * DM].rearrange("p (k c b m) -> p k c b m", k=2, c=2, b=TB)
        resid = mid[:, 6 * TB * DM:].rearrange("p (k b m) -> p k b m", k=2, b=TB)
        bf_ones = sb("bf_ones", [3, P], BF16)

        psum = ps("psum", [P, 8, 512])
        dA = psum[:, 0:4].rearrange("p (h d) t -> p h d t", h=2)
        hT = psum[:, 4:6]
        ms = psum[:, 6:8]

        par_in = sem("par_in")
        consts = sem("consts")
        prep_act = sem("prep_act")
        prep_dve = sem("prep_dve")
        x_in = sem("x_in")
        x_res_in = sem("x_res_in")
        da_ready = sem("da_ready")
        input_ready = sem("input_ready")
        scanned = sem("scanned")
        ht_ready = sem("ht_ready")
        y_added = sem("y_added")
        filled = [sem(f"filled{b}") for b in range(2)]
        freed = [sem(f"freed{b}") for b in range(2)]
        conv_first = sem("conv_first")
        conv_chain = sem("conv_chain")
        silu_done = sem("silu_done")
        sp_chain = sem("sp_chain")
        delta_done = sem("delta_done")
        du_done = sem("du_done")
        dt_in = sem("dt_in")
        z_done = sem("z_done")
        b_stored = [sem(f"b_stored{i}") for i in range(2)]
        b_in = [sem(f"b_in{g}") for g in range(N // BG)]
        gated = sem("gated")
        ln_chain = sem("ln_chain")
        rstd_done = sem("rstd_done")
        xn_done = sem("xn_done")
        stored = sem("stored")
        route_chain = sem("route_chain")
        exp_done = sem("exp_done")
        counted = sem("counted")
        scattered = sem("scattered")
        bias_in = sem("bias_in")
        bias_chain = sem("bias_chain")
        bias_stored = sem("bias_stored")
        table_chain = sem("table_chain")
        zeroed = sem("zeroed")
        w_loaded = sem("w_loaded")
        xs_in = [sem(f"xs_in{k}") for k in range(2)]
        xs_turned = sem("xs_turned")
        xs_copied = sem("xs_copied")
        gate_ready = sem("gate_ready")
        up_ready = sem("up_ready")
        gate_acted = sem("gate_acted")
        hid_ready = sem("hid_ready")
        hid_turned = sem("hid_turned")
        hid_copied = sem("hid_copied")
        down_ready = sem("down_ready")
        ys_copied = sem("ys_copied")
        ys_out = [sem(f"ys_out{k}") for k in range(2)]
        route_in = sem("route_in")
        resid_in = [sem(f"resid_in{k}") for k in range(2)]
        fetched_in = [sem(f"fetched_in{k}") for k in range(2)]
        summed = sem("summed")
        ln2_chain = sem("ln2_chain")
        rstd2_done = sem("rstd2_done")
        normed = sem("normed")
        out_stored = [sem(f"out_stored{k}") for k in range(2)]

        HALVES, PIECES = 2 * N, TB * N
        SPC = 2 * DT + 2
        RC1, RC2, RC3 = 1, 15, TB + 11
        RC = RC1 + RC2 + RC3
        TC = 29
        LN = TB + 7

        block = ctx.enter_context(nc.Block())

        def wait_copied(eng, name, s):
            eng.wait_ge(freed[BANK[name]], fills_before(name, s) + 1)

        FIRST = 3

        def block_loop(eng, step):
            with eng.Fori(0, (BLOCKS - 1 - FIRST) // 2) as i:
                for k in range(2):
                    step(2 * i + (FIRST + k), (FIRST + k) % 2)

        def sequences(eng, body):
            body(0, 0, False, True, False)
            body(1, 1, True, True, False)
            with eng.Fori(0, (SEQS - 4) // 2) as i:
                for k in range(2):
                    body(2 * i + (2 + k), k, True, True, True)
            body(SEQS - 2, 0, True, True, True)
            body(SEQS - 1, 1, True, False, True)

        @block.sync
        def _(sp):
            loads = [
                (w_in[:], W_in.rearrange("(k p) n -> p k n", p=P)),
                (w_out[:], W_out.rearrange("(k p) n -> p k n", p=P)),
                (w_x[:], W_xproj.rearrange("(k p) n -> p k n", p=P)),
                (cw[:], conv_w.rearrange("(k p) o t -> p k (o t)", p=P)),
                (cb[:], conv_b.rearrange("(k p) -> p k", p=P)),
                (wdt[:], W_dt.rearrange("o (k p) -> p (o k)", p=P)),
                (bdt[:], b_dt.rearrange("(k p) -> p k", p=P)),
                (dp[:], Dp.rearrange("(k p) -> p k", p=P)),
                (w_rt[:, 0], router_w[:, 0:P].rearrange("e p -> p e")),
                (w_rt[:, 1], router_w[:, P:DM].rearrange("e p -> p e")),
                (a_neg[:], A_log.rearrange("(o n) -> o n", o=1).to_broadcast([P, N])),
            ]
            sp.dma_start(x_sb[:], x_rows[0]).then_inc(x_in, 16)
            for dst, src in loads:
                sp.dma_start(dst, src, allow_slow_non_contiguous=True).then_inc(par_in, 16)

            def body(s, par, back, front, late):
                q = 1 - par
                if front:
                    sp.wait_ge(du_done, s + 1)
                    sp.dma_start(x_sb[:], x_rows[s + 1]).then_inc(x_in, 16)
                if back:
                    sp.wait_ge(stored, 32 * (s - 1) + 16)
                    sp.dma_start(x_res[:], x_rows[s - 1]).then_inc(x_res_in, 16)
                if isinstance(s, int) and s == SEQS:
                    sp.wait_ge(da_ready, HALVES * SEQS)
                    sp.wait_ge(input_ready, N * SEQS)
                    sp.dma_start(w_down, down_w.rearrange("e (k p) m -> p e k m", p=P)).then_inc(w_loaded, 16)
                    sp.wait_ge(ht_ready, PIECES * SEQS)
                    sp.dma_start(w_gate, gate_w.rearrange("e (k p) f -> p e k f", p=P)).then_inc(w_loaded, 16)

                def load_b(g):
                    sp.wait_ge(input_ready, N * s + BG * (g + 1))
                    if not front:
                        some = slice(E // 4 * g, E // 4 * (g + 1))
                        sp.dma_start(w_up[:, some], up_w[some].rearrange("e (k p) f -> p e k f", p=P)).then_inc(w_loaded, 16)
                        return
                    sp.dma_start(b_bc[:, BG * g:BG * (g + 1)], b_dram[q, 1 + BG * g:1 + BG * (g + 1)]
                                 .rearrange("(o n) t -> o n t", o=1).to_broadcast([P, BG, T])).then_inc(b_in[g], 16)

                if front:
                    wait_copied(sp, "bc", s)
                    sp.dma_start(b_dram[q], bc_sb[0:1 + N]).then_inc(b_stored[q], 16)
                    sp.wait_ge(b_stored[q], 16 * ((s + 1) // 2 + 1) if isinstance(s, int) else 8 * (s + 3 - q))
                    sp.dma_start(dtr[:], b_dram[q, 0:1].to_broadcast([P, T])).then_inc(dt_in, 16)
                if front or s < SEQS:
                    load_b(0)
                    load_b(1)
                if back:
                    sp.wait_ge(xn_done, TB * s)
                    sp.dma_start(xn_dram[s - 1], xn[:]).then_inc(stored, 16)
                if front or s < SEQS:
                    load_b(2)
                    load_b(3)
                if back:
                    sp.wait_ge(route_chain, RC * s)
                    sp.dma_start(route_dram[s - 1], route[:].rearrange("p c b -> p (c b)")).then_inc(stored, 16)

            for at, src in ((0, gate_b), (E * FF // P, up_b), (2 * E * FF // P, down_b)):
                rows = src.rearrange("e (f c) -> (e f) c", c=P)
                sp.dma_start(bias_f[at:at + rows.shape[0], 0], rows).then_inc(bias_in, 16)
            sp.wait_ge(consts, 9)
            half = SPARE // 2
            sp.dma_start(xs_dram[DUMP:DUMP + half * P].rearrange("(r p) m -> p r m", p=P),
                         zeros[:].to_broadcast([P, half, DM])).then_inc(stored, 16)
            sp.wait_ge(bias_chain, 5)
            sp.dma_start(bias_dram.rearrange("j (r c) -> r j c", c=P), bias_h[:]).then_inc(bias_stored, 16)
            wait_copied(sp, "bc", -1)
            sp.dma_start(b_dram[0], bc_sb[0:1 + N]).then_inc(b_stored[0], 16)
            sp.wait_ge(b_stored[0], 16)
            sp.dma_start(dtr[:], b_dram[0, 0:1].to_broadcast([P, T])).then_inc(dt_in, 16)
            for g in range(N // BG):
                sp.dma_start(b_bc[:, BG * g:BG * (g + 1)], b_dram[0, 1 + BG * g:1 + BG * (g + 1)]
                             .rearrange("(o n) t -> o n t", o=1).to_broadcast([P, BG, T])).then_inc(b_in[g], 16)
            sequences(sp, body)
            body(SEQS, 0, True, False, True)

            sp.wait_ge(stored, 32 * SEQS + 16)
            sp.dma_start(routes_flat, route_dram.rearrange("s p c -> p s c")).then_inc(route_in, 16)
            sp.wait_ge(bias_stored, 16)
            sp.dma_start(bias_w, bias_dram).then_inc(w_loaded, 16)
            sp.wait_ge(table_chain, 1)
            for e in range(E):
                end = sp.value_load(ends_i[0:1, 0, e:e + 1], min_val=0, max_val=DUMP)
                sp.dma_start(xs_dram[bass.ds(end, P)], zeros[:, 0]).then_inc(zeroed, 16)
            sp.wait_ge(zeroed, 16 * E)
            sp.wait_ge(scattered, 16 + 16 * 2 * TILES)
            sp.wait_ge(table_chain, TC)

            def load_block(j, k):
                if not (isinstance(j, int) and j < 2):
                    sp.wait_ge(xs_turned, j - 1)
                row = sp.value_load(table[0:1, 0, bass.ds(j, 1)], min_val=0, max_val=DUMP + (SPARE - 1) * P)
                sp.dma_start(xs[:, k], xs_dram[bass.ds(row, P)]).then_inc(xs_in[k], 16)

            def store_block(j, k):
                row = sp.value_load(table[0:1, 2, bass.ds(j, 1)], min_val=0, max_val=(BLOCKS - 1) * P)
                sp.wait_ge(ys_copied, j + 1)
                sp.dma_start(ys_dram[bass.ds(row, P)], ys[:, k]).then_inc(ys_out[k], 16)

            for j in range(FIRST + 1):
                load_block(j, j % 2)
            store_block(0, 0)
            block_loop(sp, lambda j, k: (load_block(j + 1, 1 - k), store_block(j - 2, k)))
            for j in range(BLOCKS - 3, BLOCKS):
                store_block(j, j % 2)
            for k in range(2):
                sp.wait_ge(ys_out[k], 16 * (BLOCKS // 2))

            def fetch(s, k):
                if not (isinstance(s, int) and s < 2):
                    sp.wait_ge(normed, TB * (s - 1))
                sp.dma_start(resid[:, k], xn_dram[s]).then_inc(resid_in[k], 16)

            def give(s, k):
                sp.wait_ge(normed, TB * (s + 1))
                sp.dma_start(out_rows[s], outs[:, k]).then_inc(out_stored[k], 16)

            for s in range(2):
                fetch(s, s)
            for s in range(SEQS):
                give(s, s % 2)
                if s + 2 < SEQS:
                    fetch(s + 2, s % 2)
            for k in range(2):
                sp.wait_ge(out_stored[k], 16 * (SEQS // 2))

        @block.gpsimd
        def _(pool):
            pool.memset(ident[:], 0.0).then_inc(consts, 1)
            pool.memset(ones[:], 1.0).then_inc(consts, 1)
            pool.memset(minus_half[:], -0.5).then_inc(consts, 1)
            pool.memset(zeros[:], 0.0).then_inc(consts, 1)
            pool.memset(bf_ones[:], 1.0).then_inc(consts, 1)
            pool.iota(falling[:, 0], pattern=[[-1, E]], base=E, channel_multiplier=0,
                      allow_small_or_imprecise_dtypes=True).then_inc(consts, 1)
            pool.iota(blocks[:, 5, 0], pattern=[[1, E]], base=0, channel_multiplier=0,
                      allow_small_or_imprecise_dtypes=True).then_inc(consts, 1)
            pool.iota(region0[:, 0], pattern=[[REGION, E]], base=0, channel_multiplier=0,
                      allow_small_or_imprecise_dtypes=True).then_inc(consts, 1)
            pool.iota(number[:, :, 0], pattern=[[1, BLOCKS]], base=0, channel_multiplier=0,
                      allow_small_or_imprecise_dtypes=True).then_inc(consts, 1)
            pool.wait_ge(consts, 9)
            pool.affine_select(out=ident[:], in_=ident[:], compare_op=ALU.not_equal, fill=1.0, base=0,
                               pattern=[[-1, P]], channel_multiplier=1).then_inc(consts, 1)
            pool.affine_select(out=before[:], in_=ones[:], compare_op=ALU.is_gt, fill=0.0, base=0,
                               pattern=[[1, P]], channel_multiplier=-1).then_inc(consts, 1)

            pool.wait_ge(consts, 11)
            half = SPARE // 2
            pool.dma_start(xs_dram[DUMP + half * P:DUMP + 2 * half * P].rearrange("(r p) m -> p r m", p=P),
                           zeros[:].to_broadcast([P, half, DM])).then_inc(scattered, 16)

            def step_size(s, q):
                pool.wait_ge(sp_chain, SPC * (s + 1))
                pool.tensor_tensor(delta[:, q], delta[:, q], du[:, q], ALU.add).then_inc(delta_done, 1)

            def times_xc(s, q):
                pool.wait_ge(delta_done, s + 1)
                pool.wait_ge(silu_done, s + 1)
                pool.tensor_tensor(du[:, q], delta[:, q], xc[:], ALU.mult).then_inc(du_done, 1)

            def gate(s, q):
                pool.wait_ge(z_done, s + 1)
                pool.wait_ge(y_added, PIECES * (s + 1))
                pool.tensor_tensor(y[:, q], y[:, q], zs[:, q], ALU.mult).then_inc(gated, 1)

            def rsqrt(s):
                pool.wait_ge(ln_chain, LN * (s + 1))
                pool.tensor_tensor(rstd[:], veps[:], minus_half[:], ALU.pow).then_inc(rstd_done, 1)

            def scatter(s, b):
                for k in range(2):
                    pool.indirect_dma_start(xs_dram, bass.IndirectOffsetOnAxis(ap=route_rows[:, k, b:b + 1], axis=0),
                                            xn[:, b], None).then_inc(scattered, 16)

            def body(s, par, back, front, late):
                for n in range(N):
                    if n % BG == 0:
                        pool.wait_ge(b_in[n // BG], 16 * (s + 1))
                    if n == 0:
                        pool.wait_ge(du_done, s + 1)
                    if n >= RING or not isinstance(s, int) or s > 0:
                        pool.wait_ge(ht_ready, PIECES * s + TB * (n - RING + 1))
                    if late and n == 3:
                        pool.wait_ge(route_chain, RC * (s - 1))
                    pool.tensor_tensor(state[:, n % RING], du[:, par], b_bc[:, n:n + 1].to_broadcast([P, DT, T]),
                                       ALU.mult).then_inc(input_ready, 1)
                    if late and 3 <= n < 3 + TB:
                        scatter(s - 2, n - 3)
                    if back and n == 2:
                        gate(s - 1, 1 - par)
                    if front and n == N - 2:
                        step_size(s + 1, 1 - par)
                    if front and n == N - 1:
                        times_xc(s + 1, 1 - par)
                    if back and n == STEP["o1"] + 4:
                        pool.wait_ge(scattered, 16 + 16 * 2 * TB * (s - 1))
                        rsqrt(s - 1)

            step_size(0, 0)
            times_xc(0, 0)
            sequences(pool, body)
            gate(SEQS - 1, (SEQS - 1) % 2)
            pool.wait_ge(route_chain, RC * (SEQS - 1))
            for b in range(TB):
                scatter(SEQS - 2, b)
            pool.wait_ge(scattered, 16 + 16 * 2 * TB * (SEQS - 1))
            rsqrt(SEQS - 1)
            pool.wait_ge(route_chain, RC * SEQS)
            for b in range(TB):
                scatter(SEQS - 1, b)

            for k in range(2):
                pool.wait_ge(ys_out[k], 16 * (BLOCKS // 2))
            for s in range(SEQS):
                k = s % 2
                pool.wait_ge(table_chain, TC)
                if s >= 2:
                    pool.wait_ge(summed, 2 * TB * (s - 1))
                for b in range(TB):
                    for c in range(2):
                        pool.indirect_dma_start(fetched[:, k, c, b], None, ys_dram,
                                                bass.IndirectOffsetOnAxis(ap=rows_out[:, s, c, b:b + 1], axis=0),
                                                ).then_inc(fetched_in[k], 16)
                if s >= 1:
                    pool.wait_ge(ln2_chain, LN * s)
                    pool.tensor_tensor(rstd[:], veps[:], minus_half[:], ALU.pow).then_inc(rstd2_done, 1)
            pool.wait_ge(ln2_chain, LN * SEQS)
            pool.tensor_tensor(rstd[:], veps[:], minus_half[:], ALU.pow).then_inc(rstd2_done, 1)

        @block.scalar
        def _(act):
            act.wait_ge(par_in, 16 * 11)
            act.activation(a_neg[:], a_neg[:], ACT.Exp).then_inc(prep_act, 1)

            def copy_in(name, s, dst, func=ACT.Copy, src=lambda bank: bank):
                b = BANK[name]
                act.wait_ge(filled[b], fills_before(name, s) + 1)
                act.activation(dst, src(ms[:, b]), func).then_inc(freed[b], 1)

            def front_at(n, s, q):
                t = s + 1
                if n == STEP["xt0"] + 2:
                    for k in range(KM):
                        copy_in(f"xt{k}", s, xT[:, k])
                for d in range(DT):
                    if n == STEP[f"in{d}"] + 2:
                        copy_in(f"in{d}", s, du[:, q, d])
                        wait_copied(act, f"in{d}", s)
                        if d == 0 and not (isinstance(s, int) and s < 0):
                            act.wait_ge(du_done, t)
                        act.activation(xc[:, d], du[:, q, d], ACT.Identity, bias=cb[:, d:d + 1],
                                       scale=cw[:, d, TAPS - 1:TAPS]).then_inc(conv_first, 1)
                if n == STEP["in3"] + 3:
                    act.wait_ge(conv_chain, (TAPS - 1) * DT * (t + 1))
                    act.activation(xc[:], xc[:], ACT.Silu).then_inc(silu_done, 1)
                for b in range(TB):
                    if n == STEP[f"z{b}"] + 2:
                        if b == 0 and not (isinstance(s, int) and s < 1):
                            act.wait_ge(gated, s)
                        copy_in(f"z{b}", s, zs[:, q, b])
                if n == STEP["bc"] + 2:
                    copy_in("bc", s, bc_sb[0:1 + 2 * N], src=lambda bank: bank[0:1 + 2 * N, :])
                if n == STEP["c"] + 2:
                    copy_in("c", s, c_sb[:, q], src=lambda bank: bank.rearrange("p (b c) -> p b c", b=TB)[:, :, 1 + N:1 + 2 * N])
                if n == STEP["bc"] + 3:
                    act.wait_ge(dt_in, 16 * (t + 1))
                    for d in range(DT):
                        act.activation(delta[:, q, d], dtr[:], ACT.Abs, bias=bdt[:, d:d + 1],
                                       scale=wdt[:, d:d + 1]).then_inc(sp_chain, 1)
                if n == STEP["bc"] + 3.5:
                    for d in range(DT):
                        act.activation(du[:, q, d], dtr[:], ACT.Relu, bias=bdt[:, d:d + 1],
                                       scale=wdt[:, d:d + 1]).then_inc(sp_chain, 1)
                if n == STEP["bc"] + 4.5:
                    act.wait_ge(sp_chain, SPC * t + DT)
                    act.activation(delta[:, q], delta[:, q], ACT.Exp, scale=-1.0).then_inc(sp_chain, 1)
                if n == STEP["bc"] + 5:
                    act.wait_ge(sp_chain, SPC * t + 2 * DT + 1)
                    act.activation(delta[:, q], delta[:, q], ACT.Ln, bias=1.0).then_inc(sp_chain, 1)
                for b in range(TB):
                    if n == STEP[f"d{b}"] + 2:
                        copy_in(f"d{b}", s, y[:, q, b])

            def back_at(n, s, q):
                for b in range(TB):
                    if n == STEP[f"g{b}"] + 2:
                        copy_in(f"g{b}", s, gT[:, b].rearrange("p k t -> p (k t)"))
                if n == STEP["rt0"] + 2:
                    for k in range(KM):
                        copy_in(f"rt{k}", s, xnT[:, k])
                if n == STEP["lg"] + 3:
                    wait_copied(act, "lg", s)
                    act.activation(prob[:], shifted[:], ACT.Exp).then_inc(exp_done, 1)

            def silu_z(s, par):
                for b in (TB - 2, TB - 1):
                    wait_copied(act, f"z{b}", s - 1)
                act.activation(zs[:, par], zs[:, par], ACT.Silu).then_inc(z_done, 1)

            def body(s, par, back, front, late):
                for n in range(N):
                    for half in range(2):
                        if half == 0 and n == 0:
                            act.wait_ge(delta_done, s + 1)
                        if n >= 1 or not isinstance(s, int) or s > 0:
                            act.wait_ge(scanned, HALVES * s + 2 * n + half - 1)
                        act.activation(dA[:, half, :, 1:T], delta[:, par, 2 * half:2 * half + 2, 1:T], ACT.Exp,
                                       scale=a_neg[:, n:n + 1]).then_inc(da_ready, 1)
                        if half == 0:
                            if back:
                                back_at(n, s, 1 - par)
                            if front:
                                front_at(n, s, 1 - par)
                            if n == 1:
                                silu_z(s, par)
                        elif front:
                            front_at(n + 0.5, s, 1 - par)
                if front:
                    front_at(N, s, 1 - par)

            for n in range(N + 1):
                front_at(n, -1, 0)
                front_at(n + 0.5, -1, 0)
            act.wait_ge(prep_dve, 3)
            sequences(act, body)
            for n in range(N):
                back_at(n, SEQS, (SEQS - 1) % 2)

            def copy_rows(j, k):
                act.wait_ge(xs_turned, j + 1)
                act.activation(xsT[:, k].rearrange("p c t -> p (c t)"), psum[:, 4 * k, 0:DM], ACT.Copy).then_inc(xs_copied, 1)

            def act_gate(j, k):
                act.wait_ge(gate_ready, j + 1)
                act.activation(gate_act[:, k], psum[:, 4 * k + 1], ACT.Silu).then_inc(gate_acted, 1)

            def copy_hidden(j, k):
                act.wait_ge(hid_turned, j + 1)
                act.activation(hidT[:, k].rearrange("p c t -> p (c t)"), psum[:, 4 * k + 3], ACT.Copy).then_inc(hid_copied, 1)

            def step(j, k, last=False):
                act_gate(j, k)
                if not (isinstance(j, int) and j == 0):
                    copy_hidden(j - 1, 1 - k)
                if not last:
                    copy_rows(j + 1, 1 - k)

            copy_rows(0, 0)
            for j in range(FIRST):
                step(j, j % 2)
            block_loop(act, step)
            step(BLOCKS - 1, (BLOCKS - 1) % 2, last=True)
            copy_hidden(BLOCKS - 1, (BLOCKS - 1) % 2)

        @block.vector
        def _(dve):
            dve.wait_ge(consts, 11)
            dve.wait_ge(par_in, 16 * 11)
            dve.wait_ge(prep_act, 1)
            dve.tensor_scalar(a_neg[:], a_neg[:], -1.0, None, ALU.mult).then_inc(prep_dve, 1)
            for h in range(2):
                dve.memset(dA[:, h, :, 0:1], 0.0).then_inc(prep_dve, 1)
            dve.memset(bc_sb[:], 0.0).then_inc(prep_dve, 1)
            for d in range(DT):
                dve.tensor_scalar(diag_d[:, d], ident[:], dp[:, d:d + 1], None, ALU.mult).then_inc(prep_dve, 1)
            dve.tensor_copy(base[:, TB:TB + 1], region0[:]).then_inc(prep_dve, 1)
            dve.wait_ge(bias_in, 16 * 3)
            dve.tensor_copy(bias_h[:, 0], bias_f[:, 0]).then_inc(bias_chain, 1)
            dve.wait_ge(bias_chain, 1)
            dve.tensor_tensor(bias_f[:, 1], bias_f[:, 0], bias_h[:, 0], ALU.subtract).then_inc(bias_chain, 1)
            dve.wait_ge(bias_chain, 2)
            dve.tensor_copy(bias_h[:, 1], bias_f[:, 1]).then_inc(bias_chain, 1)
            dve.wait_ge(bias_chain, 3)
            dve.tensor_tensor(bias_f[:, 0], bias_f[:, 1], bias_h[:, 1], ALU.subtract).then_inc(bias_chain, 1)
            dve.wait_ge(bias_chain, 4)
            dve.tensor_copy(bias_h[:, 2], bias_f[:, 0]).then_inc(bias_chain, 1)

            def front_at(n, s, q):
                for d in range(DT):
                    if n == STEP[f"in{d}"] + 1:
                        dve.wait_ge(conv_first, DT * (s + 1) + d + 1)
                        for j in range(1, TAPS):
                            if j > 1:
                                dve.wait_ge(conv_chain, (TAPS - 1) * (DT * (s + 1) + d) + j - 1)
                            dve.scalar_tensor_tensor(xc[:, d, j:T], du[:, q, d, 0:T - j], cw[:, d, TAPS - 1 - j:TAPS - j],
                                                     xc[:, d, j:T], ALU.mult, ALU.add).then_inc(conv_chain, 1)

            def moments(chain, at):
                dve.wait_ge(chain, at + TB)
                dve.tensor_tensor(mean2[:], stats[:, :, 1], stats[:, :, 4], ALU.add).then_inc(chain, 1)
                dve.tensor_tensor(apart[:], stats[:, :, 1], stats[:, :, 4], ALU.subtract).then_inc(chain, 1)
                dve.tensor_tensor(squares[:], stats[:, :, 2], stats[:, :, 5], ALU.add).then_inc(chain, 1)
                dve.wait_ge(chain, at + TB + 3)
                dve.tensor_tensor(apart[:], apart[:], apart[:], ALU.mult).then_inc(chain, 1)
                dve.tensor_scalar(mean[:], mean2[:], 0.5, None, ALU.mult).then_inc(chain, 1)
                dve.tensor_scalar(squares[:], squares[:], 1.0 / DM, EPS, ALU.mult, ALU.add).then_inc(chain, 1)
                dve.wait_ge(chain, at + TB + 6)
                dve.scalar_tensor_tensor(veps[:], apart[:], 0.25, squares[:], ALU.mult, ALU.add).then_inc(chain, 1)

            def back_at(n, s):
                r = s - 1
                for h in range(2):
                    if n == STEP[f"o{h}"] + 1:
                        if h == 0:
                            dve.wait_ge(x_res_in, 16 * s)
                        b = BANK[f"o{h}"]
                        dve.wait_ge(filled[b], fills_before(f"o{h}", s) + 1)
                        dve.tensor_tensor(res[:, 2 * h:2 * h + 2].rearrange("p b m -> p (b m)"), ms[:, b],
                                          x_res[:, 2 * h:2 * h + 2].rearrange("p b m -> p (b m)"), ALU.add).then_inc(freed[b], 1)
                if n == STEP["o1"] + 1:
                    for b in range(TB):
                        dve.wait_ge(freed[BANK[f"o{b // 2}"]], fills_before(f"o{b // 2}", s) + 1)
                        dve.bn_stats(stats[:, b], res[:, b]).then_inc(ln_chain, 1)
                    moments(ln_chain, LN * r)
                if n == STEP["o1"] + 3:
                    dve.wait_ge(rstd_done, r + 1)
                    for b in range(TB):
                        dve.tensor_scalar(xn[:, b], res[:, b], mean[:, b:b + 1], rstd[:, b:b + 1],
                                          ALU.subtract, ALU.mult).then_inc(xn_done, 1)

            def route_at(n, s):
                r = s - 1
                at = RC * r
                wide = [P, TB, E]
                logits = ms[:, BANK["lg"], 0:TB * E].rearrange("p (b e) -> p b e", e=E)
                first_of = falling[:].to_broadcast(wide)
                if n == STEP["lg"] + 1:
                    dve.wait_ge(filled[BANK["lg"]], fills_before("lg", s) + 1)
                    dve.tensor_reduce(top[:, 0, :, 0], logits, X, ALU.max).then_inc(route_chain, 1)
                    dve.wait_ge(route_chain, at + 1)
                    dve.tensor_tensor(shifted[:], logits, top[:, 0].to_broadcast(wide), ALU.subtract).then_inc(freed[BANK["lg"]], 1)
                if n == STEP["lg"] + 2:
                    at = at + RC1
                    dve.wait_ge(exp_done, r + 1)
                    steps = [
                        lambda: dve.tensor_reduce(top[:, 1, :, 0], prob[:], X, ALU.add),
                        lambda: dve.reciprocal(top[:, 2], top[:, 1]),
                        lambda: dve.tensor_tensor(prob[:], prob[:], top[:, 2].to_broadcast(wide), ALU.mult),
                    ]
                    for m, make in enumerate(steps):
                        if m:
                            dve.wait_ge(route_chain, at + m)
                        make().then_inc(route_chain, 1)
                    at = at + 3
                    for c, left in ((0, prob), (1, equal)):
                        dve.wait_ge(route_chain, at + 6 * c)
                        dve.tensor_reduce(top[:, 3 + c, :, 0], left[:], X, ALU.max).then_inc(route_chain, 1)
                        dve.wait_ge(route_chain, at + 6 * c + 1)
                        dve.tensor_tensor(both[:], left[:], top[:, 3 + c].to_broadcast(wide), ALU.is_equal).then_inc(route_chain, 1)
                        dve.wait_ge(route_chain, at + 6 * c + 2)
                        dve.tensor_tensor(both[:], both[:], first_of, ALU.mult).then_inc(route_chain, 1)
                        dve.wait_ge(route_chain, at + 6 * c + 3)
                        dve.tensor_reduce(top[:, 5, :, 0], both[:], X, ALU.max).then_inc(route_chain, 1)
                        dve.wait_ge(route_chain, at + 6 * c + 4)
                        dve.tensor_tensor(pick[:, c], first_of, top[:, 5].to_broadcast(wide), ALU.is_equal).then_inc(route_chain, 1)
                        dve.wait_ge(route_chain, at + 6 * c + 5)
                        if c == 0:
                            dve.scalar_tensor_tensor(equal[:], pick[:, 0], -2.0, prob[:], ALU.mult, ALU.add).then_inc(route_chain, 1)
                        else:
                            dve.tensor_tensor(both[:], pick[:, 0], pick[:, 1], ALU.add).then_inc(route_chain, 1)
                if n == STEP["pf"] + 1:
                    at = at + RC1 + RC2
                    bank = ms[:, BANK["pf"]]
                    ahead = bank[:, 0:TB * E].rearrange("p (b e) -> p b e", e=E)
                    total = bank[:, TB * E:2 * TB * E].rearrange("p (b e) -> p b e", e=E)
                    dve.wait_ge(filled[BANK["pf"]], fills_before("pf", s) + 1)
                    dve.tensor_copy(base[:, 0], base[:, TB]).then_inc(route_chain, 1)
                    for b in range(TB):
                        dve.wait_ge(route_chain, at + b + 1)
                        dve.tensor_tensor(base[:, b + 1], base[:, b], total[:, b], ALU.add).then_inc(route_chain, 1)
                    dve.wait_ge(route_chain, at + TB + 1)
                    dve.tensor_tensor(row_of[:], ahead, base[:, 0:TB], ALU.add).then_inc(freed[BANK["pf"]], 1)
                    wait_copied(dve, "pf", s)
                    dve.tensor_tensor(equal[:], row_of[:], pick[:, 0], ALU.mult).then_inc(route_chain, 1)
                    dve.tensor_tensor(shifted[:], row_of[:], pick[:, 1], ALU.mult).then_inc(route_chain, 1)
                    dve.tensor_tensor(top[:, 6], top[:, 3], top[:, 4], ALU.add).then_inc(route_chain, 1)
                    at = at + TB + 4
                    dve.wait_ge(route_chain, at)
                    dve.tensor_reduce(rows_f[:, 0], equal[:], X, ALU.add).then_inc(route_chain, 1)
                    dve.tensor_reduce(rows_f[:, 1], shifted[:], X, ALU.add).then_inc(route_chain, 1)
                    dve.tensor_scalar(top[:, 6], top[:, 6], 1e-9, None, ALU.add).then_inc(route_chain, 1)
                    dve.wait_ge(route_chain, at + 3)
                    dve.tensor_copy(route_rows, rows_f[:]).then_inc(route_chain, 1)
                    dve.reciprocal(top[:, 7], top[:, 6]).then_inc(route_chain, 1)
                    dve.wait_ge(route_chain, at + 5)
                    dve.tensor_tensor(route[:, 2], top[:, 3, :, 0], top[:, 7, :, 0], ALU.mult).then_inc(route_chain, 1)
                    dve.tensor_tensor(route[:, 3], top[:, 4, :, 0], top[:, 7, :, 0], ALU.mult).then_inc(route_chain, 1)

            def add_state(s, n, b, par):
                dve.wait_ge(ht_ready, PIECES * s + TB * n + b + 1)
                if n > 0:
                    dve.wait_ge(y_added, PIECES * s + TB * (n - 1) + b + 1)
                dve.scalar_tensor_tensor(y[:, par, b], hT[:, b % 2], c_sb[:, par, b, n:n + 1], y[:, par, b],
                                         ALU.mult, ALU.add).then_inc(y_added, 1)

            def body(s, par, back, front, late):
                for n in range(N):
                    for half in range(2):
                        dve.wait_ge(da_ready, HALVES * s + 2 * n + half + 1)
                        if half == 0:
                            dve.wait_ge(input_ready, N * s + n + 1)
                        v = state[:, n % RING, 2 * half:2 * half + 2].rearrange("p d t -> p (d t)")
                        dve.tensor_tensor_scan(v, dA[:, half].rearrange("p d t -> p (d t)"), v, 0.0,
                                               ALU.mult, ALU.add).then_inc(scanned, 1)
                        for b in (2 * half, 2 * half + 1):
                            if n > 0:
                                add_state(s, n - 1, b, par)
                            elif back:
                                add_state(s - 1, N - 1, b, 1 - par)
                    if back:
                        back_at(n, s)
                        route_at(n, s)
                    if front:
                        front_at(n, s, 1 - par)

            for n in range(N + 1):
                front_at(n, -1, 0)
            sequences(dve, body)
            for b in range(TB):
                add_state(SEQS - 1, N - 1, b, (SEQS - 1) % 2)
            for n in range(N):
                back_at(n, SEQS)
                route_at(n, SEQS)

            count = [0]

            def chain(ins):
                count[0] += 1
                ins.then_inc(table_chain, 1)
                dve.wait_ge(table_chain, count[0])

            grid = [P, BLOCKS, E]
            used, n_blocks, end, start, offset, expert = (blocks[:, m] for m in range(6))
            dve.wait_ge(route_chain, RC * SEQS)
            chain(dve.tensor_copy(ends_i[:], base[:, TB:TB + 1]))
            chain(dve.tensor_tensor(used, base[:, TB:TB + 1], region0[:], ALU.subtract))
            chain(dve.tensor_scalar(used_i[:], used, float(P - 1), None, ALU.add))
            chain(dve.tensor_scalar(used_i[:], used_i[:], P.bit_length() - 1, None, ALU.arith_shift_right))
            chain(dve.tensor_copy(n_blocks, used_i[:]))
            chain(dve.tensor_tensor_scan(end[:, 0], ones[:, 0:E], n_blocks[:, 0], 0.0, ALU.mult, ALU.add))
            chain(dve.tensor_tensor(start, end, n_blocks, ALU.subtract))
            chain(dve.scalar_tensor_tensor(offset, start, -float(P), region0[:], ALU.mult, ALU.add))
            numbers = number[:].to_broadcast(grid)
            chain(dve.tensor_tensor(inside[:, 0], numbers, start.to_broadcast(grid), ALU.is_ge))
            chain(dve.tensor_tensor(inside[:, 1], numbers, end.to_broadcast(grid), ALU.is_lt))
            chain(dve.tensor_tensor(inside[:, 0], inside[:, 0], inside[:, 1], ALU.mult))
            chain(dve.tensor_reduce(sums[:, 0], inside[:, 0], X, ALU.add))
            chain(dve.tensor_tensor(inside[:, 1], inside[:, 0], expert.to_broadcast(grid), ALU.mult))
            chain(dve.tensor_reduce(sums[:, 1], inside[:, 1], X, ALU.add))
            chain(dve.tensor_tensor(inside[:, 1], inside[:, 0], offset.to_broadcast(grid), ALU.mult))
            chain(dve.tensor_reduce(sums[:, 2], inside[:, 1], X, ALU.add))
            chain(dve.tensor_scalar(sums[:, 3], sums[:, 0], -float(DUMP - 2 * TOK), float(DUMP - 2 * TOK), ALU.mult, ALU.add))
            chain(dve.tensor_tensor(sums[:, 3], sums[:, 3], sums[:, 2], ALU.add))
            chain(dve.scalar_tensor_tensor(table[:, 0], number[:, :, 0], float(P), sums[:, 3], ALU.mult, ALU.add))
            chain(dve.tensor_copy(table[:, 1], sums[:, 1]))
            chain(dve.tensor_scalar(table[:, 2], number[:, :, 0], float(P), None, ALU.mult))
            shape = [P, SEQS * 2 * TB, E]
            rows_in = routes[:, :, 0:2].bitcast(U32)
            in_region, weighed = (inside[:, m, 0:shape[1]] for m in range(2))
            flat = rows_f2.rearrange("p s c b -> p (s c b)")
            chain(dve.tensor_copy(end[:, :, 1:E], offset[:, :, 0:E - 1]))
            chain(dve.memset(end[:, :, 0:1], 0.0))
            chain(dve.tensor_tensor(end, offset, end, ALU.subtract))
            dve.wait_ge(route_in, 16)
            chain(dve.tensor_copy(rows_f2, rows_in))
            chain(dve.tensor_tensor(in_region, xc[:, 2, 0:shape[1]].rearrange("p (r o) -> p r o", o=1).to_broadcast(shape), region0[:].to_broadcast(shape), ALU.is_ge))
            chain(dve.tensor_tensor(weighed, in_region, end.to_broadcast(shape), ALU.mult))
            chain(dve.tensor_reduce(sums[:, 0, 0:shape[1]], weighed, X, ALU.add))
            chain(dve.tensor_tensor(rows_out.rearrange("p s c b -> p (s c b)"), flat, sums[:, 0, 0:shape[1]], ALU.subtract))
            assert count[0] == TC

            def gate_up(j, k):
                dve.wait_ge(up_ready, j + 1)
                dve.wait_ge(gate_acted, j + 1)
                dve.tensor_tensor(hid[:, k], gate_act[:, k], psum[:, 4 * k + 2], ALU.mult).then_inc(hid_ready, 1)

            def copy_result(j, k):
                dve.wait_ge(down_ready, j + 1)
                if not (isinstance(j, int) and j < 2):
                    dve.wait_ge(ys_out[k], 16 * (j // 2) if isinstance(j, int) else 8 * (j - k))
                dve.tensor_copy(ys[:, k], psum[:, 4 * k, DM:2 * DM]).then_inc(ys_copied, 1)

            def step(j, k):
                gate_up(j, k)
                if not (isinstance(j, int) and j == 0):
                    copy_result(j - 1, 1 - k)

            for j in range(FIRST):
                step(j, j % 2)
            block_loop(dve, step)
            step(BLOCKS - 1, (BLOCKS - 1) % 2)
            copy_result(BLOCKS - 1, (BLOCKS - 1) % 2)

            for s in range(SEQS):
                k = s % 2
                at = LN * s
                dve.wait_ge(fetched_in[k], 16 * 2 * TB * (s // 2 + 1))
                dve.wait_ge(resid_in[k], 16 * (s // 2 + 1))
                for c in range(2):
                    for b in range(TB):
                        if c:
                            dve.wait_ge(summed, 2 * TB * s + b + 1)
                        dve.scalar_tensor_tensor(resid[:, k, b], fetched[:, k, c, b], routes[:, s, 2 + c, b:b + 1], resid[:, k, b],
                                                 ALU.mult, ALU.add).then_inc(summed, 1)
                for b in range(TB):
                    dve.wait_ge(summed, 2 * TB * s + TB + b + 1)
                    dve.bn_stats(stats[:, b], resid[:, k, b]).then_inc(ln2_chain, 1)
                moments(ln2_chain, at)
                dve.wait_ge(rstd2_done, s + 1)
                if s >= 2:
                    dve.wait_ge(out_stored[k], 16 * (s // 2))
                for b in range(TB):
                    dve.tensor_scalar(outs[:, k, b], resid[:, k, b], mean[:, b:b + 1], rstd[:, b:b + 1],
                                      ALU.subtract, ALU.mult).then_inc(normed, 1)

        @block.tensor
        def _(pe):
            pe.wait_ge(consts, 11)
            pe.wait_ge(par_in, 16 * 11)
            pe.wait_ge(prep_dve, 4 + DT)

            def fill(name, s):
                b, before_ = BANK[name], fills_before(name, s)
                if not (isinstance(before_, int) and before_ == 0):
                    pe.wait_ge(freed[b], before_)
                return ms[:, b]

            def front_at(n, s, q):
                t = s + 1
                if n == STEP["xt0"]:
                    pe.wait_ge(x_in, 16 * (t + 1))
                    for k in range(KM):
                        bank = fill(f"xt{k}", s)
                        for b in range(TB):
                            ins = pe.transpose(bank[:, b * P:(b + 1) * P], x_sb[:, b, k * P:(k + 1) * P], ident[:])
                        ins.then_inc(filled[BANK[f"xt{k}"]], 1)
                for d in range(DT):
                    if n == STEP[f"in{d}"]:
                        for k in range(KM):
                            wait_copied(pe, f"xt{k}", s)
                        bank = fill(f"in{d}", s)
                        for k in range(KM):
                            ins = pe.matmul(bank, w_in[:, k, d * P:(d + 1) * P], xT[:, k], start=k == 0, stop=k == KM - 1)
                        ins.then_inc(filled[BANK[f"in{d}"]], 1)
                for b in range(TB):
                    if n == STEP[f"z{b}"]:
                        bank = fill(f"z{b}", s)
                        for k in range(KM):
                            ins = pe.matmul(bank, xT[:, k, b * P:(b + 1) * P], w_in[:, k, DI:2 * DI], start=k == 0, stop=k == KM - 1)
                        ins.then_inc(filled[BANK[f"z{b}"]], 1)
                if n == STEP["bc"]:
                    pe.wait_ge(silu_done, t + 1)
                    bank = fill("bc", s)
                    for k in range(DT):
                        ins = pe.matmul(bank[0:1 + 2 * N, :], w_x[:, k], xc[:, k], start=k == 0, stop=k == DT - 1)
                    ins.then_inc(filled[BANK["bc"]], 1)
                if n == STEP["c"]:
                    wait_copied(pe, "bc", s)
                    bank = fill("c", s)
                    for b in range(TB):
                        ins = pe.transpose(bank[:, b * P:(b + 1) * P], bc_sb[:, b * P:(b + 1) * P], ident[:])
                    ins.then_inc(filled[BANK["c"]], 1)
                for b in range(TB):
                    if n == STEP[f"d{b}"]:
                        bank = fill(f"d{b}", s)
                        for k in range(DT):
                            ins = pe.matmul(bank[:, k * P:(k + 1) * P], xc[:, k, b * P:(b + 1) * P], diag_d[:, k], start=True, stop=True)
                        ins.then_inc(filled[BANK[f"d{b}"]], 1)

            def back_at(n, s, q):
                for b in range(TB):
                    if n == STEP[f"g{b}"]:
                        pe.wait_ge(gated, s)
                        bank = fill(f"g{b}", s)
                        for k in range(DT):
                            ins = pe.transpose(bank[:, k * P:(k + 1) * P], y[:, q, b, k * P:(k + 1) * P], ident[:])
                        ins.then_inc(filled[BANK[f"g{b}"]], 1)
                for h in range(2):
                    if n == STEP[f"o{h}"]:
                        for b in range(2 * h, 2 * h + 2):
                            wait_copied(pe, f"g{b}", s)
                        bank = fill(f"o{h}", s)
                        for b in range(2 * h, 2 * h + 2):
                            for k in range(DT):
                                ins = pe.matmul(bank[:, (b % 2) * DM:(b % 2 + 1) * DM], gT[:, b, k], w_out[:, k],
                                                start=k == 0, stop=k == DT - 1)
                        ins.then_inc(filled[BANK[f"o{h}"]], 1)
                if n == STEP["rt0"]:
                    pe.wait_ge(xn_done, TB * s)
                    for k in range(KM):
                        bank = fill(f"rt{k}", s)
                        for b in range(TB):
                            ins = pe.transpose(bank[:, b * P:(b + 1) * P], xn[:, b, k * P:(k + 1) * P], ident[:])
                        ins.then_inc(filled[BANK[f"rt{k}"]], 1)
                if n == STEP["lg"]:
                    bank = fill("lg", s)
                    for k in range(KM):
                        wait_copied(pe, f"rt{k}", s)
                    for b in range(TB):
                        for k in range(KM):
                            ins = pe.matmul(bank[:, b * E:(b + 1) * E], xnT[:, k, b * P:(b + 1) * P], w_rt[:, k],
                                            start=k == 0, stop=k == KM - 1)
                    ins.then_inc(filled[BANK["lg"]], 1)
                if n == STEP["pf"]:
                    pe.wait_ge(route_chain, RC * (s - 1) + RC1 + RC2)
                    bank = fill("pf", s)
                    picks = both[:].rearrange("p b e -> p (b e)")
                    pe.matmul(bank[:, 0:TB * E], before[:], picks, start=True, stop=True)
                    ins = pe.matmul(bank[:, TB * E:2 * TB * E], ones[:], picks, start=True, stop=True)
                    ins.then_inc(filled[BANK["pf"]], 1)

            def body(s, par, back, front, late):
                for n in range(N):
                    pe.wait_ge(scanned, HALVES * s + 2 * n + 2)
                    for b in range(TB):
                        at = TB * n + b
                        if at >= 2 or not isinstance(s, int) or s > 0:
                            pe.wait_ge(y_added, PIECES * s + at - 1)
                        for d in range(DT):
                            ins = pe.transpose(hT[:, b % 2, d * P:(d + 1) * P], state[:, n % RING, d, b * P:(b + 1) * P], ident[:])
                        ins.then_inc(ht_ready, 1)
                        if b == 1:
                            if back:
                                back_at(n, s, 1 - par)
                            if front:
                                front_at(n, s, 1 - par)

            for n in range(N):
                front_at(n, -1, 0)
            sequences(pe, body)
            for n in range(N):
                back_at(n, SEQS, (SEQS - 1) % 2)

            pe.wait_ge(table_chain, TC)
            pe.wait_ge(w_loaded, 16 * 7)

            def expert_of(j):
                return pe.value_load(table[0:1, 1, bass.ds(j, 1)], min_val=0, max_val=E - 1)

            def turn_rows(j, k):
                pe.wait_ge(xs_in[k], 16 * (j // 2 + 1) if isinstance(j, int) else 8 * (j - k) + 16)
                if not (isinstance(j, int) and j < 4):
                    pe.wait_ge(ys_copied, j - 3)
                for c in range(KM):
                    ins = pe.transpose(psum[:, 4 * k, c * P:(c + 1) * P], xs[:, k, c * P:(c + 1) * P], ident[:])
                ins.then_inc(xs_turned, 1)

            def project(j, k, e, bank, w, bias, signal):
                for c in range(KM):
                    pe.matmul(psum[:, bank], xsT[:, k, c], w[:, bass.ds(e, 1), c].rearrange("p o f -> p (o f)"), start=c == 0, stop=False)
                pe.matmul(psum[:, bank], bf_ones[:], bias[:, bass.ds(e, 1)].rearrange("p o f -> p (o f)"),
                          start=False, stop=True).then_inc(signal, 1)

            def gate(j, k, e):
                pe.wait_ge(xs_copied, j + 1)
                if not (isinstance(j, int) and j < 2):
                    pe.wait_ge(gate_acted, j - 1)
                project(j, k, e, 4 * k + 1, w_gate, g_bias, gate_ready)

            def up(j, k, e):
                if not (isinstance(j, int) and j < 2):
                    pe.wait_ge(hid_ready, j - 1)
                project(j, k, e, 4 * k + 2, w_up, u_bias, up_ready)

            def turn_hidden(j, k):
                pe.wait_ge(hid_ready, j + 1)
                if not (isinstance(j, int) and j < 2):
                    pe.wait_ge(hid_copied, j - 1)
                for c in range(FB):
                    ins = pe.transpose(psum[:, 4 * k + 3, c * P:(c + 1) * P], hid[:, k, c * P:(c + 1) * P], ident[:])
                ins.then_inc(hid_turned, 1)

            def down(j, k, e):
                pe.wait_ge(hid_copied, j + 1)
                if isinstance(j, int) and j + 2 >= BLOCKS:
                    pe.wait_ge(xs_copied, BLOCKS)
                else:
                    pe.wait_ge(xs_copied, j + 3)
                if not (isinstance(j, int) and j < 2):
                    pe.wait_ge(ys_copied, j - 1)
                result = psum[:, 4 * k, DM:2 * DM]
                for c in range(FB):
                    pe.matmul(result, hidT[:, k, c], w_down[:, bass.ds(e, 1), c].rearrange("p o m -> p (o m)"), start=c == 0, stop=False)
                pe.matmul(result, bf_ones[:], d_bias[:, bass.ds(e, 1)].rearrange("p o m -> p (o m)"),
                          start=False, stop=True).then_inc(down_ready, 1)

            def step(j, k, last=False):
                e = expert_of(j)
                gate(j, k, e)
                more = not (isinstance(j, int) and j == 0)
                if more:
                    turn_hidden(j - 1, 1 - k)
                if not last:
                    turn_rows(j + 1, 1 - k)
                up(j, k, e)
                if more:
                    down(j - 1, 1 - k, expert_of(j - 1))

            turn_rows(0, 0)
            for j in range(FIRST):
                step(j, j % 2)
            block_loop(pe, step)
            step(BLOCKS - 1, (BLOCKS - 1) % 2, last=True)
            turn_hidden(BLOCKS - 1, (BLOCKS - 1) % 2)
            down(BLOCKS - 1, (BLOCKS - 1) % 2, expert_of(BLOCKS - 1))


_INS = ['L0_attn_x', 'L0_attn_W_in', 'L0_attn_conv_w', 'L0_attn_conv_b', 'L0_attn_W_xproj', 'L0_attn_W_dt',
        'L0_attn_b_dt', 'L0_attn_A_log', 'L0_attn_Dp', 'L0_attn_W_out', 'L0_ffn_router_w', 'L0_ffn_gate_w',
        'L0_ffn_gate_b', 'L0_ffn_up_w', 'L0_ffn_up_b', 'L0_ffn_down_w', 'L0_ffn_down_b']
_OUTS = [((SEQS, T, DM), 'float32')]


def kernel(**inputs):
    import numpy as _np
    import concourse.bacc as _bacc
    from concourse import mybir as _mybir
    from concourse.bass_utils import run_bass_kernel_spmd as _run

    nc = _bacc.Bacc("TRN2", target_bir_lowering=False, num_devices=1)
    arrays, args = {}, []
    for name in _INS:
        a = _np.ascontiguousarray(inputs[name])
        arrays[f"in_{name}_dram"] = a
        args.append(nc.dram_tensor(f"in_{name}_dram", a.shape, _mybir.dt.from_np(a.dtype), kind="ExternalInput").ap())
    for i, (shape, dtype) in enumerate(_OUTS):
        dt = _mybir.dt.from_np(_np.dtype(dtype))
        args.append(nc.dram_tensor(f"out_{i}_dram", shape, dt, kind="ExternalOutput").ap())
    mamba_moe_program(nc, *args)
    r = _run(nc, [arrays], core_ids=[0])
    return r.results[0]["out_0_dram"]
```

```python
from contextlib import ExitStack

import concourse.bass as bass
from concourse import mybir

ALU = mybir.AluOpType
ACT = mybir.ActivationFunctionType
F32 = mybir.dt.float32
I32 = mybir.dt.int32
U32 = mybir.dt.uint32
X = mybir.AxisListType.X

P = 128
SEQS, T, DM = 8, 512, 256
DI, N, TAPS = 512, 16, 4
E, FF = 8, 512
TB = T // P
DT = DI // P
KM = DM // P
FB = FF // P
TILES = SEQS * TB
TOK = SEQS * T
RING = 4
BG = 4
REGION = TOK + P
DUMP = E * REGION
BLOCKS = 2 * TOK // P + E - 1
BLOCKS += BLOCKS % 2
SPARE = BLOCKS - 2 * TOK // P
EPS = 1e-5

USES = [
    ("xt0", "front", 0, 0), ("xt1", "front", 1, 0), ("in0", "front", 0, 1), ("z0", "front", 1, 1),
    ("in1", "front", 0, 2), ("g0", "back", 1, 2), ("in2", "front", 0, 3), ("g1", "back", 1, 3),
    ("in3", "front", 0, 4), ("g2", "back", 1, 4), ("g3", "back", 1, 5), ("o0", "back", 0, 5),
    ("o1", "back", 1, 6), ("bc", "front", 0, 7), ("z1", "front", 1, 7), ("c", "front", 0, 8),
    ("z2", "front", 1, 8), ("z3", "front", 0, 9), ("d0", "front", 1, 9), ("rt0", "back", 0, 10),
    ("rt1", "back", 1, 10), ("lg", "back", 0, 11), ("d1", "front", 1, 12), ("d2", "front", 1, 13),
    ("pf", "back", 0, 14), ("d3", "front", 1, 14),
]
BANK = {name: bank for name, _, bank, _ in USES}
STEP = {name: step for name, _, _, step in USES}
PER = {(kind, b): sum(k == kind and bank == b for _, k, bank, _ in USES) for kind in ("front", "back") for b in (0, 1)}


def fills_before(name, s):
    b = BANK[name]
    at = [u[0] for u in USES].index(name)
    fixed = isinstance(s, int)
    kinds = [k for k, there in (("back", not fixed or s >= 1), ("front", not fixed or s <= SEQS - 2)) if there]
    here = sum(k in kinds and bank == b for _, k, bank, _ in USES[:at])
    if fixed:
        return PER["front", b] * min(s + 1, SEQS) + PER["back", b] * max(s - 1, 0) + here
    return (PER["front", b] + PER["back", b]) * s + (PER["front", b] - PER["back", b] + here)


def mamba_moe_program(nc, x, W_in, conv_w, conv_b, W_xproj, W_dt, b_dt, A_log, Dp, W_out,
                      router_w, gate_w, gate_b, up_w, up_b, down_w, down_b, out):
    x_rows = x.rearrange("s (b p) m -> s p b m", p=P)
    out_rows = out.rearrange("s (b p) m -> s p b m", p=P)
    xn_dram = nc.dram_tensor("xn_scratch", (SEQS, P, TB, DM), F32).ap()
    b_dram = nc.dram_tensor("b_scratch", (2, 1 + N, T), F32).ap()
    xs_dram = nc.dram_tensor("expert_in", (DUMP + SPARE * P, DM), F32).ap()
    ys_dram = nc.dram_tensor("expert_out", (BLOCKS * P, DM), F32).ap()
    route_dram = nc.dram_tensor("route_scratch", (SEQS, P, 4 * TB), F32).ap()

    with ExitStack() as ctx:
        def sb(name, shape, dt=F32):
            return ctx.enter_context(nc.sbuf_tensor(name, shape, dt))

        def ps(name, shape, dt=F32):
            return ctx.enter_context(nc.psum_tensor(name, shape, dt))

        def sem(name):
            return ctx.enter_context(nc.semaphore(name))

        ident = sb("ident", [P, P])
        before = sb("before", [P, P])
        ones = sb("ones", [P, P])
        front_a = sb("front_a", [P, E * FF])
        front_b = sb("front_b", [P, E * FF])
        w_in = front_a[:, 0:KM * 2 * DI].rearrange("p (k n) -> p k n", k=KM)
        x_sb = front_a[:, KM * 2 * DI:KM * 2 * DI + TB * DM].rearrange("p (b m) -> p b m", b=TB)
        xT = front_a[:, KM * 2 * DI + TB * DM:].rearrange("p (k t) -> p k t", k=KM)
        xc = front_b[:, 0:DT * T].rearrange("p (d t) -> p d t", d=DT)
        dtr = front_b[:, DT * T:(DT + 1) * T]
        bc_sb = front_b[:, (DT + 1) * T:(DT + 2) * T]
        diag_d = front_b[:, (DT + 2) * T:(DT + 2) * T + DT * P].rearrange("p (k c) -> p k c", k=DT)
        w_out = sb("w_out", [P, DT, DM])
        w_x = sb("w_x", [P, DT, 2 * N + 1])
        w_rt = sb("w_rt", [P, KM, E])
        cw = sb("cw", [P, DT, TAPS])
        cb = sb("cb", [P, DT])
        wdt = sb("wdt", [P, DT])
        bdt = sb("bdt", [P, DT])
        dp = sb("dp", [P, DT])
        a_neg = sb("a_neg", [P, N])
        minus_half = sb("minus_half", [P, TB])
        x_res = sb("x_res", [P, TB, DM])
        big = sb("big", [P, 3 * E * KM * FF])
        per = RING * DT * T
        state = big[:, 0:per].rearrange("p (r d t) -> p r d t", r=RING, d=DT)
        b_bc = big[:, per:2 * per].rearrange("p (n t) -> p n t", n=N)
        delta = big[:, 2 * per:5 * per // 2].rearrange("p (q d t) -> p q d t", q=2, d=DT)
        du = big[:, 5 * per // 2:3 * per].rearrange("p (q d t) -> p q d t", q=2, d=DT)
        mid = sb("mid", [P, 4 * TB * DI])
        zs = mid[:, 0:2 * TB * DI].rearrange("p (q b n) -> p q b n", q=2, b=TB)
        xn_last = zs[:, 0, :, 0:DM]
        y = mid[:, 2 * TB * DI:].rearrange("p (q b n) -> p q b n", q=2, b=TB)
        c_sb = sb("c_sb", [P, 2, TB, N])
        gT = sb("gT", [P, TB, DT, P])
        res = sb("res", [P, TB, DM])
        xn = sb("xn", [P, TB, DM])
        xnT = sb("xnT", [P, KM, T])
        stats = sb("stats", [P, TB, 6])
        mean2 = sb("mean2", [P, TB])
        neg_mean = sb("neg_mean", [P, TB])
        shift = sb("shift", [P, TB])
        apart = sb("apart", [P, TB])
        squares = sb("squares", [P, TB])
        veps = sb("veps", [P, TB])
        rstd = sb("rstd", [P, TB])
        root = sb("root", [P, TB])
        falling = sb("falling", [P, 1, E])
        region0 = sb("region0", [P, 1, E])
        shifted = sb("shifted", [P, TB, E])
        prob = sb("prob", [P, TB, E])
        equal = sb("equal", [P, TB, E])
        pick = sb("pick", [P, 2, TB, E])
        both = sb("both", [P, TB, E])
        base = sb("base", [P, TB + 1, E])
        row_of = sb("row_of", [P, TB, E])
        top = sb("top", [P, 8, TB, 1])
        rows_f = sb("rows_f", [P, 2, TB])
        route = sb("route", [P, 4, TB])
        route_rows = route[:, 0:2].bitcast(U32)
        zeros = sb("zeros", [P, 1, DM])
        blocks = sb("blocks", [P, 6, 1, E])
        used_i = sb("used_i", [P, 1, E], I32)
        ends_i = sb("ends_i", [P, 1, E], I32)
        number = sb("number", [P, BLOCKS, 1])
        inside = gT[:].rearrange("p b k t -> p (b k t)")[:, 0:2 * BLOCKS * E].rearrange("p (m j e) -> p m j e", m=2, e=E)
        sums = sb("sums", [P, 4, BLOCKS])
        table = sb("table", [P, 3, BLOCKS], I32)

        w_gate = big[:, 0:E * KM * FF].rearrange("p (e k f) -> p e k f", e=E, k=KM)
        w_up = big[:, E * KM * FF:2 * E * KM * FF].rearrange("p (e k f) -> p e k f", e=E, k=KM)
        w_down = big[:, 2 * E * KM * FF:].rearrange("p (e k m) -> p e k m", e=E, k=FB)
        u_bias = front_a[:].rearrange("p (e f) -> p e f", e=E)
        g_bias = front_b[:].rearrange("p (e f) -> p e f", e=E)
        d_bias = sb("d_bias", [P, E, DM])
        xs = mid[:, 0:512].rearrange("p (k m) -> p k m", k=2)
        xsT = mid[:, 512:1024].rearrange("p (k c t) -> p k c t", k=2, c=KM)
        gate_act = mid[:, 1024:2048].rearrange("p (k f) -> p k f", k=2)
        hid = mid[:, 2048:3072].rearrange("p (k f) -> p k f", k=2)
        ys = mid[:, 3072:3584].rearrange("p (k m) -> p k m", k=2)
        hidT = gT[:, 0:2]
        routes_flat = xnT[:, 0, 0:SEQS * 4 * TB].rearrange("p (s c) -> p s c", s=SEQS)
        routes = xnT[:, 0, 0:SEQS * 4 * TB].rearrange("p (s c b) -> p s c b", s=SEQS, c=4)
        rows_flat = xnT[:, 1, 0:SEQS * 2 * TB]
        rows_f2 = rows_flat.rearrange("p (s c b) -> p s c b", s=SEQS, c=2)
        rows_out = xnT[:, 1, SEQS * 2 * TB:SEQS * 4 * TB].bitcast(U32).rearrange("p (s c b) -> p s c b", s=SEQS, c=2)
        outs = mid[:, 0:2 * TB * DM].rearrange("p (k b m) -> p k b m", k=2, b=TB)
        fetched = mid[:, 2 * TB * DM:6 * TB * DM].rearrange("p (k c b m) -> p k c b m", k=2, c=2, b=TB)
        resid = mid[:, 6 * TB * DM:].rearrange("p (k b m) -> p k b m", k=2, b=TB)

        psum = ps("psum", [P, 8, 512])
        dA = psum[:, 0:4].rearrange("p (h d) t -> p h d t", h=2)
        hT = psum[:, 4:6]
        ms = psum[:, 6:8]

        w_in_in = sem("w_in_in")
        conv_in = sem("conv_in")
        par_in = sem("par_in")
        PARAMS = 8
        consts = sem("consts")
        prep_act = sem("prep_act")
        prep_dve = sem("prep_dve")
        x_in = sem("x_in")
        x_res_in = sem("x_res_in")
        da_ready = sem("da_ready")
        input_ready = sem("input_ready")
        scanned = sem("scanned")
        ht_ready = sem("ht_ready")
        y_added = sem("y_added")
        filled = [sem(f"filled{b}") for b in range(2)]
        freed = [sem(f"freed{b}") for b in range(2)]
        conv_first = sem("conv_first")
        conv_chain = sem("conv_chain")
        silu_done = sem("silu_done")
        sp_chain = sem("sp_chain")
        delta_done = sem("delta_done")
        du_done = sem("du_done")
        dt_in = sem("dt_in")
        z_done = sem("z_done")
        b_stored = [sem(f"b_stored{i}") for i in range(2)]
        b_in = [sem(f"b_in{g}") for g in range(N // BG)]
        gated = sem("gated")
        ln_chain = sem("ln_chain")
        rstd_done = sem("rstd_done")
        xn_done = sem("xn_done")
        stored = sem("stored")
        route_chain = sem("route_chain")
        exp_done = sem("exp_done")
        scattered = sem("scattered")
        table_chain = sem("table_chain")
        zeroed = sem("zeroed")
        w_loaded = sem("w_loaded")
        bias_loaded = sem("bias_loaded")
        xs_in = [sem(f"xs_in{k}") for k in range(2)]
        xs_turned = sem("xs_turned")
        xs_copied = sem("xs_copied")
        gate_ready = sem("gate_ready")
        up_ready = sem("up_ready")
        gate_biased = sem("gate_biased")
        up_biased = sem("up_biased")
        gate_acted = sem("gate_acted")
        hid_ready = sem("hid_ready")
        hid_turned = sem("hid_turned")
        hid_copied = sem("hid_copied")
        down_ready = sem("down_ready")
        ys_copied = sem("ys_copied")
        ys_out = [sem(f"ys_out{k}") for k in range(2)]
        route_in = sem("route_in")
        resid_in = [sem(f"resid_in{k}") for k in range(2)]
        fetched_in = [sem(f"fetched_in{k}") for k in range(2)]
        summed = sem("summed")
        ln2_chain = sem("ln2_chain")
        rooted = sem("rooted")
        rstd2_done = sem("rstd2_done")
        normed = sem("normed")
        out_stored = [sem(f"out_stored{k}") for k in range(2)]

        HALVES, PIECES = 2 * N, TB * N
        SPC = 2 * DT + 2
        RC1, RC2, RC3 = 1, 15, TB + 11
        RC = RC1 + RC2 + RC3
        TC1, TC2 = 21, 8
        LN = TB + 7

        block = ctx.enter_context(nc.Block())

        def xn_of(s):
            return xn_last if isinstance(s, int) and s == SEQS else xn

        def wait_copied(eng, name, s):
            eng.wait_ge(freed[BANK[name]], fills_before(name, s) + 1)

        FIRST = 3

        def block_loop(eng, step):
            with eng.Fori(0, (BLOCKS - 1 - FIRST) // 2) as i:
                before = None
                for k in range(2):
                    before = step(2 * i + (FIRST + k), (FIRST + k) % 2, before)

        def sequences(eng, body):
            body(0, 0, False, True, False)
            body(1, 1, True, True, False)
            with eng.Fori(0, (SEQS - 4) // 2) as i:
                for k in range(2):
                    body(2 * i + (2 + k), k, True, True, True)
            body(SEQS - 2, 0, True, True, True)
            body(SEQS - 1, 1, True, False, True)

        @block.sync
        def _(sp):
            sp.dma_start(x_sb, x_rows[0]).then_inc(x_in, 16)
            sp.dma_start(w_in, W_in.rearrange("(k p) n -> p k n", p=P)).then_inc(w_in_in, 16)
            loads = [
                (conv_in, cw[:], conv_w.rearrange("(k p) o t -> p k (o t)", p=P)),
                (conv_in, cb[:], conv_b.rearrange("(k p) -> p k", p=P)),
                (par_in, wdt[:], W_dt.rearrange("o (k p) -> p (o k)", p=P)),
                (par_in, bdt[:], b_dt.rearrange("(k p) -> p k", p=P)),
                (par_in, dp[:], Dp.rearrange("(k p) -> p k", p=P)),
                (par_in, a_neg[:], A_log.rearrange("(o n) -> o n", o=1).to_broadcast([P, N])),
                (par_in, w_x[:], W_xproj.rearrange("(k p) n -> p k n", p=P)),
                (par_in, w_out[:], W_out.rearrange("(k p) n -> p k n", p=P)),
                (par_in, w_rt[:, 0], router_w[:, 0:P].rearrange("e p -> p e")),
                (par_in, w_rt[:, 1], router_w[:, P:DM].rearrange("e p -> p e")),
            ]
            for signal, dst, src in loads:
                sp.dma_start(dst, src, allow_slow_non_contiguous=True).then_inc(signal, 16)

            def body(s, par, back, front, late):
                q = 1 - par
                if front:
                    sp.wait_ge(du_done, s + 1)
                    sp.dma_start(x_sb[:], x_rows[s + 1]).then_inc(x_in, 16)
                if back:
                    sp.wait_ge(stored, 32 * (s - 1) + 16)
                    sp.dma_start(x_res[:], x_rows[s - 1]).then_inc(x_res_in, 16)
                if isinstance(s, int) and s == SEQS:
                    sp.wait_ge(da_ready, HALVES * SEQS)
                    sp.wait_ge(input_ready, N * SEQS)
                    sp.dma_start(w_down, down_w.rearrange("e (k p) m -> p e k m", p=P)).then_inc(w_loaded, 16)
                    sp.wait_ge(ht_ready, PIECES * SEQS)
                    sp.dma_start(w_gate, gate_w.rearrange("e (k p) f -> p e k f", p=P)).then_inc(w_loaded, 16)

                def load_b(g):
                    sp.wait_ge(input_ready, N * s + BG * (g + 1))
                    if not front:
                        some = slice(E // 4 * g, E // 4 * (g + 1))
                        sp.dma_start(w_up[:, some], up_w[some].rearrange("e (k p) f -> p e k f", p=P)).then_inc(w_loaded, 16)
                        return
                    sp.dma_start(b_bc[:, BG * g:BG * (g + 1)], b_dram[q, 1 + BG * g:1 + BG * (g + 1)]
                                 .rearrange("(o n) t -> o n t", o=1).to_broadcast([P, BG, T])).then_inc(b_in[g], 16)

                if front:
                    wait_copied(sp, "bc", s)
                    sp.dma_start(b_dram[q], bc_sb[0:1 + N]).then_inc(b_stored[q], 16)
                    sp.wait_ge(b_stored[q], 16 * ((s + 1) // 2 + 1) if isinstance(s, int) else 8 * (s + 3 - q))
                    sp.dma_start(dtr[:], b_dram[q, 0:1].to_broadcast([P, T])).then_inc(dt_in, 16)
                if isinstance(s, int) and s == SEQS - 1:
                    sp.wait_ge(du_done, SEQS)
                    sp.wait_ge(freed[BANK["d3"]], fills_before("d3", s - 1) + 1)
                    sp.wait_ge(freed[BANK["z3"]], fills_before("z3", s - 1) + 1)
                    for dst, src in ((u_bias, up_b), (g_bias, gate_b), (d_bias[:], down_b)):
                        sp.dma_start(dst, src.rearrange("(o e) f -> o e f", o=1).to_broadcast(dst.shape)).then_inc(bias_loaded, 16)
                if front or s < SEQS:
                    load_b(0)
                    load_b(1)
                if back:
                    sp.wait_ge(xn_done, TB * s)
                    sp.dma_start(xn_dram[s - 1], xn_of(s)[:, :]).then_inc(stored, 16)
                if front or s < SEQS:
                    load_b(2)
                    load_b(3)
                if back:
                    sp.wait_ge(route_chain, RC * s)
                    sp.dma_start(route_dram[s - 1], route[:].rearrange("p c b -> p (c b)")).then_inc(stored, 16)

            sp.wait_ge(consts, 8)
            half = SPARE // 2
            sp.dma_start(xs_dram[DUMP:DUMP + half * P].rearrange("(r p) m -> p r m", p=P),
                         zeros[:].to_broadcast([P, half, DM])).then_inc(stored, 16)
            wait_copied(sp, "bc", -1)
            sp.dma_start(b_dram[0], bc_sb[0:1 + N]).then_inc(b_stored[0], 16)
            sp.wait_ge(b_stored[0], 16)
            sp.dma_start(dtr[:], b_dram[0, 0:1].to_broadcast([P, T])).then_inc(dt_in, 16)
            for g in range(N // BG):
                sp.dma_start(b_bc[:, BG * g:BG * (g + 1)], b_dram[0, 1 + BG * g:1 + BG * (g + 1)]
                             .rearrange("(o n) t -> o n t", o=1).to_broadcast([P, BG, T])).then_inc(b_in[g], 16)
            sequences(sp, body)
            body(SEQS, 0, True, False, True)

            sp.wait_ge(stored, 32 * SEQS + 16)
            sp.dma_start(routes_flat, route_dram.rearrange("s p c -> p s c")).then_inc(route_in, 16)
            sp.wait_ge(table_chain, 1)
            for e in range(E):
                end = sp.value_load(ends_i[0:1, 0, e:e + 1], min_val=0, max_val=DUMP)
                sp.dma_start(xs_dram[bass.ds(end, P)], zeros[:, 0]).then_inc(zeroed, 16)
            sp.wait_ge(zeroed, 16 * E)
            sp.wait_ge(scattered, 16 + 16 * 2 * TILES)
            sp.wait_ge(table_chain, TC1)

            def load_block(j, k):
                if not (isinstance(j, int) and j < 2):
                    sp.wait_ge(xs_turned, j - 1)
                row = sp.value_load(table[0:1, 0, bass.ds(j, 1)], min_val=0, max_val=DUMP + (SPARE - 1) * P)
                sp.dma_start(xs[:, k], xs_dram[bass.ds(row, P)]).then_inc(xs_in[k], 16)

            def store_block(j, k):
                row = sp.value_load(table[0:1, 2, bass.ds(j, 1)], min_val=0, max_val=(BLOCKS - 1) * P)
                sp.wait_ge(ys_copied, j + 1)
                sp.dma_start(ys_dram[bass.ds(row, P)], ys[:, k]).then_inc(ys_out[k], 16)

            for j in range(FIRST + 1):
                load_block(j, j % 2)
            store_block(0, 0)
            block_loop(sp, lambda j, k, _: (load_block(j + 1, 1 - k), store_block(j - 2, k)))
            for j in range(BLOCKS - 3, BLOCKS):
                store_block(j, j % 2)
            for k in range(2):
                sp.wait_ge(ys_out[k], 16 * (BLOCKS // 2))

            def fetch(s, k):
                if not (isinstance(s, int) and s < 2):
                    sp.wait_ge(normed, TB * (s - 1))
                sp.dma_start(resid[:, k], xn_dram[s]).then_inc(resid_in[k], 16)

            def give(s, k):
                sp.wait_ge(normed, TB * (s + 1))
                sp.dma_start(out_rows[s], outs[:, k]).then_inc(out_stored[k], 16)

            for s in range(2):
                fetch(s, s)
            for s in range(SEQS):
                give(s, s % 2)
                if s + 2 < SEQS:
                    fetch(s + 2, s % 2)
            for k in range(2):
                sp.wait_ge(out_stored[k], 16 * (SEQS // 2))

        @block.gpsimd
        def _(pool):
            pool.memset(ident[:], 0.0).then_inc(consts, 1)
            pool.memset(ones[:], 1.0).then_inc(consts, 1)
            pool.memset(minus_half[:], -0.5).then_inc(consts, 1)
            pool.memset(zeros[:], 0.0).then_inc(consts, 1)
            pool.iota(falling[:, 0], pattern=[[-1, E]], base=E, channel_multiplier=0,
                      allow_small_or_imprecise_dtypes=True).then_inc(consts, 1)
            pool.iota(blocks[:, 5, 0], pattern=[[1, E]], base=0, channel_multiplier=0,
                      allow_small_or_imprecise_dtypes=True).then_inc(consts, 1)
            pool.iota(region0[:, 0], pattern=[[REGION, E]], base=0, channel_multiplier=0,
                      allow_small_or_imprecise_dtypes=True).then_inc(consts, 1)
            pool.iota(number[:, :, 0], pattern=[[1, BLOCKS]], base=0, channel_multiplier=0,
                      allow_small_or_imprecise_dtypes=True).then_inc(consts, 1)
            pool.wait_ge(consts, 8)
            pool.affine_select(out=ident[:], in_=ident[:], compare_op=ALU.not_equal, fill=1.0, base=0,
                               pattern=[[-1, P]], channel_multiplier=1).then_inc(consts, 1)
            pool.affine_select(out=before[:], in_=ones[:], compare_op=ALU.is_gt, fill=0.0, base=0,
                               pattern=[[1, P]], channel_multiplier=-1).then_inc(consts, 1)

            pool.wait_ge(consts, 10)
            half = SPARE // 2
            pool.dma_start(xs_dram[DUMP + half * P:DUMP + 2 * half * P].rearrange("(r p) m -> p r m", p=P),
                           zeros[:].to_broadcast([P, half, DM])).then_inc(scattered, 16)

            def add_softplus(s, q):
                pool.wait_ge(sp_chain, SPC * (s + 1))
                pool.tensor_tensor(delta[:, q], delta[:, q], du[:, q], ALU.add).then_inc(delta_done, 1)

            def times_xc(s, q):
                pool.wait_ge(delta_done, s + 1)
                pool.wait_ge(silu_done, s + 1)
                pool.tensor_tensor(du[:, q], delta[:, q], xc[:], ALU.mult).then_inc(du_done, 1)

            def gate(s, q):
                pool.wait_ge(z_done, s + 1)
                pool.wait_ge(y_added, PIECES * (s + 1))
                pool.tensor_tensor(y[:, q], y[:, q], zs[:, q], ALU.mult).then_inc(gated, 1)

            def rsqrt(s):
                pool.wait_ge(ln_chain, LN * (s + 1))
                pool.tensor_tensor(rstd[:], veps[:], minus_half[:], ALU.pow).then_inc(rstd_done, 1)
                pool.wait_ge(rstd_done, 2 * s + 1)
                pool.tensor_tensor(shift[:], neg_mean[:], rstd[:], ALU.mult).then_inc(rstd_done, 1)

            def scatter(s, b):
                for k in range(2):
                    pool.indirect_dma_start(xs_dram, bass.IndirectOffsetOnAxis(ap=route_rows[:, k, b:b + 1], axis=0),
                                            xn_of(s + 1)[:, b], None).then_inc(scattered, 16)

            def body(s, par, back, front, late):
                for n in range(N):
                    if n % BG == 0:
                        pool.wait_ge(b_in[n // BG], 16 * (s + 1))
                    if n == 0:
                        pool.wait_ge(du_done, s + 1)
                    if n >= RING or not isinstance(s, int) or s > 0:
                        pool.wait_ge(ht_ready, PIECES * s + TB * (n - RING + 1))
                    if late and n == 3:
                        pool.wait_ge(route_chain, RC * (s - 1))
                    pool.tensor_tensor(state[:, n % RING], du[:, par], b_bc[:, n:n + 1].to_broadcast([P, DT, T]),
                                       ALU.mult).then_inc(input_ready, 1)
                    if late and 3 <= n < 3 + TB:
                        scatter(s - 2, n - 3)
                    if back and n == 2:
                        gate(s - 1, 1 - par)
                    if front and n == N - 2:
                        add_softplus(s + 1, 1 - par)
                    if front and n == N - 1:
                        times_xc(s + 1, 1 - par)
                    if back and n == STEP["o1"] + 4:
                        pool.wait_ge(scattered, 16 + 16 * 2 * TB * (s - 1))
                        rsqrt(s - 1)

            sequences(pool, body)
            pool.wait_ge(route_chain, RC * (SEQS - 1))
            for b in range(TB):
                scatter(SEQS - 2, b)
            rsqrt(SEQS - 1)
            pool.wait_ge(route_chain, RC * SEQS)
            for b in range(TB):
                scatter(SEQS - 1, b)

            for k in range(2):
                pool.wait_ge(ys_out[k], 16 * (BLOCKS // 2))
            for s in range(SEQS):
                k = s % 2
                pool.wait_ge(table_chain, TC1 + TC2)
                if s >= 2:
                    pool.wait_ge(summed, 2 * TB * (s - 1))
                for b in range(TB):
                    for c in range(2):
                        pool.indirect_dma_start(fetched[:, k, c, b], None, ys_dram,
                                                bass.IndirectOffsetOnAxis(ap=rows_out[:, s, c, b:b + 1], axis=0),
                                                ).then_inc(fetched_in[k], 16)

        @block.scalar
        def _(act):
            act.wait_ge(conv_in, 16 * 2)

            def copy_in(name, s, dst, func=ACT.Copy, src=lambda bank: bank):
                b = BANK[name]
                act.wait_ge(filled[b], fills_before(name, s) + 1)
                act.activation(dst, src(ms[:, b]), func).then_inc(freed[b], 1)

            def front_at(n, s, q):
                t = s + 1
                if n == STEP["xt0"] + 2:
                    for k in range(KM):
                        copy_in(f"xt{k}", s, xT[:, k])
                for d in range(DT):
                    if n == STEP[f"in{d}"] + 2:
                        copy_in(f"in{d}", s, du[:, q, d])
                        wait_copied(act, f"in{d}", s)
                        if d == 0 and not (isinstance(s, int) and s < 0):
                            act.wait_ge(du_done, t)
                        act.activation(xc[:, d], du[:, q, d], ACT.Identity, bias=cb[:, d:d + 1],
                                       scale=cw[:, d, TAPS - 1:TAPS]).then_inc(conv_first, 1)
                if n == STEP["in3"] + 3:
                    act.wait_ge(conv_chain, (TAPS - 1) * DT * (t + 1))
                    act.activation(xc[:], xc[:], ACT.Silu).then_inc(silu_done, 1)
                for b in range(TB):
                    if n == STEP[f"z{b}"] + 2:
                        if b == 0 and not (isinstance(s, int) and s < 1):
                            act.wait_ge(gated, s)
                        copy_in(f"z{b}", s, zs[:, q, b])
                if n == STEP["bc"] + 2:
                    copy_in("bc", s, bc_sb[0:1 + 2 * N], src=lambda bank: bank[0:1 + 2 * N, :])
                if n == STEP["c"] + 2:
                    copy_in("c", s, c_sb[:, q], src=lambda bank: bank.rearrange("p (b c) -> p b c", b=TB)[:, :, 1 + N:1 + 2 * N])
                if n == STEP["bc"] + 3:
                    act.wait_ge(dt_in, 16 * (t + 1))
                    for d in range(DT):
                        act.activation(delta[:, q, d], dtr[:], ACT.Abs, bias=bdt[:, d:d + 1],
                                       scale=wdt[:, d:d + 1]).then_inc(sp_chain, 1)
                if n == STEP["bc"] + 4:
                    for d in range(DT):
                        act.activation(du[:, q, d], dtr[:], ACT.Relu, bias=bdt[:, d:d + 1],
                                       scale=wdt[:, d:d + 1]).then_inc(sp_chain, 1)
                if n == STEP["bc"] + 5:
                    act.wait_ge(sp_chain, SPC * t + DT)
                    act.activation(delta[:, q], delta[:, q], ACT.Exp, scale=-1.0).then_inc(sp_chain, 1)
                if n == STEP["bc"] + 6:
                    act.wait_ge(sp_chain, SPC * t + 2 * DT + 1)
                    act.activation(delta[:, q], delta[:, q], ACT.Ln, bias=1.0).then_inc(sp_chain, 1)
                for b in range(TB):
                    if n == STEP[f"d{b}"] + 2:
                        copy_in(f"d{b}", s, y[:, q, b])

            def back_at(n, s, q):
                for b in range(TB):
                    if n == STEP[f"g{b}"] + 2:
                        copy_in(f"g{b}", s, gT[:, b].rearrange("p k t -> p (k t)"))
                if n == STEP["o1"] + 3.5:
                    act.wait_ge(rstd_done, 2 * s)
                    for b in range(TB):
                        act.activation(xn_of(s)[:, b], res[:, b], ACT.Identity, bias=shift[:, b:b + 1],
                                       scale=rstd[:, b:b + 1]).then_inc(xn_done, 1)
                if n == STEP["rt0"] + 2:
                    for k in range(KM):
                        copy_in(f"rt{k}", s, xnT[:, k])
                if n == STEP["lg"] + 3:
                    wait_copied(act, "lg", s)
                    act.activation(prob[:], shifted[:], ACT.Exp).then_inc(exp_done, 1)

            def silu_z(s, par):
                for b in (TB - 2, TB - 1):
                    wait_copied(act, f"z{b}", s - 1)
                act.activation(zs[:, par], zs[:, par], ACT.Silu).then_inc(z_done, 1)

            def body(s, par, back, front, late):
                for n in range(N):
                    for half in range(2):
                        if half == 0 and n == 0:
                            act.wait_ge(delta_done, s + 1)
                        if n >= 1 or not isinstance(s, int) or s > 0:
                            act.wait_ge(scanned, HALVES * s + 2 * n + half - 1)
                        act.activation(dA[:, half, :, 1:T], delta[:, par, 2 * half:2 * half + 2, 1:T], ACT.Exp,
                                       scale=a_neg[:, n:n + 1]).then_inc(da_ready, 1)
                        if half == 0:
                            if back:
                                back_at(n, s, 1 - par)
                            if front:
                                front_at(n, s, 1 - par)
                            if n == (2 if isinstance(s, int) and s == 0 else 0):
                                silu_z(s, par)
                        else:
                            if back:
                                back_at(n + 0.5, s, 1 - par)
                            if front:
                                front_at(n + 0.5, s, 1 - par)
                if front:
                    front_at(N, s, 1 - par)

            for n in range(N + 1):
                front_at(n, -1, 0)
                if n == STEP["bc"]:
                    act.wait_ge(par_in, 16 * PARAMS)
                front_at(n + 0.5, -1, 0)
            act.activation(a_neg[:], a_neg[:], ACT.Exp).then_inc(prep_act, 1)
            act.wait_ge(prep_dve, 4 + DT + 1)
            sequences(act, body)
            for n in range(N):
                back_at(n, SEQS, (SEQS - 1) % 2)
                back_at(n + 0.5, SEQS, (SEQS - 1) % 2)

            def copy_rows(j, k):
                act.wait_ge(xs_turned, j + 1)
                act.activation(xsT[:, k].rearrange("p c t -> p (c t)"), psum[:, 4 * k, 0:DM], ACT.Copy).then_inc(xs_copied, 1)

            def act_gate(j, k):
                act.wait_ge(gate_biased, j + 1)
                act.activation(gate_act[:, k], gate_act[:, k], ACT.Silu).then_inc(gate_acted, 1)

            def copy_hidden(j, k):
                act.wait_ge(hid_turned, j + 1)
                act.activation(hidT[:, k].rearrange("p c t -> p (c t)"), psum[:, 4 * k + 3], ACT.Copy).then_inc(hid_copied, 1)

            def step(j, k, _, last=False):
                if not (isinstance(j, int) and j == 0):
                    copy_hidden(j - 1, 1 - k)
                if not last:
                    copy_rows(j + 1, 1 - k)
                act_gate(j, k)

            copy_rows(0, 0)
            for j in range(FIRST):
                step(j, j % 2, None)
            block_loop(act, step)
            step(BLOCKS - 1, (BLOCKS - 1) % 2, None, last=True)
            copy_hidden(BLOCKS - 1, (BLOCKS - 1) % 2)

            for s in range(SEQS):
                act.wait_ge(ln2_chain, LN * (s + 1))
                if s >= 1:
                    act.wait_ge(rstd2_done, s)
                act.activation(root[:], veps[:], ACT.Sqrt).then_inc(rooted, 1)

        @block.vector
        def _(dve):
            dve.wait_ge(consts, 10)
            for h in range(2):
                dve.memset(dA[:, h, :, 0:1], 0.0).then_inc(prep_dve, 1)
            dve.memset(bc_sb[:], 0.0).then_inc(prep_dve, 1)
            dve.wait_ge(par_in, 16 * PARAMS)
            for d in range(DT):
                dve.tensor_scalar(diag_d[:, d], ident[:], dp[:, d:d + 1], None, ALU.mult).then_inc(prep_dve, 1)
            dve.tensor_copy(base[:, TB:TB + 1], region0[:]).then_inc(prep_dve, 1)
            def front_at(n, s, q):
                for d in range(DT):
                    if n == STEP[f"in{d}"] + 1:
                        dve.wait_ge(conv_first, DT * (s + 1) + d + 1)
                        for j in range(1, TAPS):
                            if j > 1:
                                dve.wait_ge(conv_chain, (TAPS - 1) * (DT * (s + 1) + d) + j - 1)
                            dve.scalar_tensor_tensor(xc[:, d, j:T], du[:, q, d, 0:T - j], cw[:, d, TAPS - 1 - j:TAPS - j],
                                                     xc[:, d, j:T], ALU.mult, ALU.add).then_inc(conv_chain, 1)

            def moments(chain, at):
                dve.wait_ge(chain, at + TB)
                dve.tensor_tensor(mean2[:], stats[:, :, 1], stats[:, :, 4], ALU.add).then_inc(chain, 1)
                dve.tensor_tensor(apart[:], stats[:, :, 1], stats[:, :, 4], ALU.subtract).then_inc(chain, 1)
                dve.tensor_tensor(squares[:], stats[:, :, 2], stats[:, :, 5], ALU.add).then_inc(chain, 1)
                dve.wait_ge(chain, at + TB + 3)
                dve.tensor_tensor(apart[:], apart[:], apart[:], ALU.mult).then_inc(chain, 1)
                dve.tensor_scalar(neg_mean[:], mean2[:], -0.5, None, ALU.mult).then_inc(chain, 1)
                dve.tensor_scalar(squares[:], squares[:], 1.0 / DM, EPS, ALU.mult, ALU.add).then_inc(chain, 1)
                dve.wait_ge(chain, at + TB + 6)
                dve.scalar_tensor_tensor(veps[:], apart[:], 0.25, squares[:], ALU.mult, ALU.add).then_inc(chain, 1)

            def back_at(n, s):
                r = s - 1
                for h in range(2):
                    if n == STEP[f"o{h}"] + 1:
                        if h == 0:
                            dve.wait_ge(x_res_in, 16 * s)
                            if not (isinstance(s, int) and s < 2):
                                dve.wait_ge(xn_done, TB * (s - 1))
                        b = BANK[f"o{h}"]
                        dve.wait_ge(filled[b], fills_before(f"o{h}", s) + 1)
                        dve.tensor_tensor(res[:, 2 * h:2 * h + 2].rearrange("p b m -> p (b m)"), ms[:, b],
                                          x_res[:, 2 * h:2 * h + 2].rearrange("p b m -> p (b m)"), ALU.add).then_inc(freed[b], 1)
                if n == STEP["o1"] + 1:
                    for b in range(TB):
                        dve.wait_ge(freed[BANK[f"o{b // 2}"]], fills_before(f"o{b // 2}", s) + 1)
                        dve.bn_stats(stats[:, b], res[:, b]).then_inc(ln_chain, 1)
                    moments(ln_chain, LN * r)

            def route_at(n, s):
                r = s - 1
                at = RC * r
                wide = [P, TB, E]
                logits = ms[:, BANK["lg"], 0:TB * E].rearrange("p (b e) -> p b e", e=E)
                first_of = falling[:].to_broadcast(wide)
                if n == STEP["lg"] + 1:
                    dve.wait_ge(filled[BANK["lg"]], fills_before("lg", s) + 1)
                    dve.tensor_reduce(top[:, 0, :, 0], logits, X, ALU.max).then_inc(route_chain, 1)
                    dve.wait_ge(route_chain, at + 1)
                    dve.tensor_tensor(shifted[:], logits, top[:, 0].to_broadcast(wide), ALU.subtract).then_inc(freed[BANK["lg"]], 1)
                if n == STEP["lg"] + 2:
                    at = at + RC1
                    dve.wait_ge(exp_done, r + 1)
                    dve.tensor_reduce(top[:, 1, :, 0], prob[:], X, ALU.add).then_inc(route_chain, 1)
                    dve.wait_ge(route_chain, at + 1)
                    dve.reciprocal(top[:, 2], top[:, 1]).then_inc(route_chain, 1)
                    dve.wait_ge(route_chain, at + 2)
                    dve.tensor_tensor(prob[:], prob[:], top[:, 2].to_broadcast(wide), ALU.mult).then_inc(route_chain, 1)
                    at = at + 3
                    for c, left in ((0, prob), (1, equal)):
                        dve.wait_ge(route_chain, at + 6 * c)
                        dve.tensor_reduce(top[:, 3 + c, :, 0], left[:], X, ALU.max).then_inc(route_chain, 1)
                        dve.wait_ge(route_chain, at + 6 * c + 1)
                        dve.tensor_tensor(both[:], left[:], top[:, 3 + c].to_broadcast(wide), ALU.is_equal).then_inc(route_chain, 1)
                        dve.wait_ge(route_chain, at + 6 * c + 2)
                        dve.tensor_tensor(both[:], both[:], first_of, ALU.mult).then_inc(route_chain, 1)
                        dve.wait_ge(route_chain, at + 6 * c + 3)
                        dve.tensor_reduce(top[:, 5, :, 0], both[:], X, ALU.max).then_inc(route_chain, 1)
                        dve.wait_ge(route_chain, at + 6 * c + 4)
                        dve.tensor_tensor(pick[:, c], first_of, top[:, 5].to_broadcast(wide), ALU.is_equal).then_inc(route_chain, 1)
                        dve.wait_ge(route_chain, at + 6 * c + 5)
                        if c == 0:
                            dve.scalar_tensor_tensor(equal[:], pick[:, 0], -2.0, prob[:], ALU.mult, ALU.add).then_inc(route_chain, 1)
                        else:
                            dve.tensor_tensor(both[:], pick[:, 0], pick[:, 1], ALU.add).then_inc(route_chain, 1)
                if n == STEP["pf"] + 1:
                    at = at + RC1 + RC2
                    bank = ms[:, BANK["pf"]]
                    ahead = bank[:, 0:TB * E].rearrange("p (b e) -> p b e", e=E)
                    total = bank[:, TB * E:2 * TB * E].rearrange("p (b e) -> p b e", e=E)
                    dve.wait_ge(filled[BANK["pf"]], fills_before("pf", s) + 1)
                    dve.tensor_copy(base[:, 0], base[:, TB]).then_inc(route_chain, 1)
                    for b in range(TB):
                        dve.wait_ge(route_chain, at + b + 1)
                        dve.tensor_tensor(base[:, b + 1], base[:, b], total[:, b], ALU.add).then_inc(route_chain, 1)
                    dve.wait_ge(route_chain, at + TB + 1)
                    dve.tensor_tensor(row_of[:], ahead, base[:, 0:TB], ALU.add).then_inc(freed[BANK["pf"]], 1)
                    wait_copied(dve, "pf", s)
                    dve.tensor_tensor(equal[:], row_of[:], pick[:, 0], ALU.mult).then_inc(route_chain, 1)
                    dve.tensor_tensor(shifted[:], row_of[:], pick[:, 1], ALU.mult).then_inc(route_chain, 1)
                    dve.tensor_tensor(top[:, 6], top[:, 3], top[:, 4], ALU.add).then_inc(route_chain, 1)
                    at = at + TB + 4
                    dve.wait_ge(route_chain, at)
                    dve.tensor_reduce(rows_f[:, 0], equal[:], X, ALU.add).then_inc(route_chain, 1)
                    dve.tensor_reduce(rows_f[:, 1], shifted[:], X, ALU.add).then_inc(route_chain, 1)
                    dve.tensor_scalar(top[:, 6], top[:, 6], 1e-9, None, ALU.add).then_inc(route_chain, 1)
                    dve.wait_ge(route_chain, at + 3)
                    if isinstance(s, int) and s == SEQS:
                        dve.wait_ge(scattered, 16 + 16 * 2 * TB * (SEQS - 1))
                    dve.tensor_copy(route_rows, rows_f[:]).then_inc(route_chain, 1)
                    dve.reciprocal(top[:, 7], top[:, 6]).then_inc(route_chain, 1)
                    dve.wait_ge(route_chain, at + 5)
                    dve.tensor_tensor(route[:, 2], top[:, 3, :, 0], top[:, 7, :, 0], ALU.mult).then_inc(route_chain, 1)
                    dve.tensor_tensor(route[:, 3], top[:, 4, :, 0], top[:, 7, :, 0], ALU.mult).then_inc(route_chain, 1)

            def add_state(s, n, b, par):
                dve.wait_ge(ht_ready, PIECES * s + TB * n + b + 1)
                if n > 0:
                    dve.wait_ge(y_added, PIECES * s + TB * (n - 1) + b + 1)
                dve.scalar_tensor_tensor(y[:, par, b], hT[:, b % 2], c_sb[:, par, b, n:n + 1], y[:, par, b],
                                         ALU.mult, ALU.add).then_inc(y_added, 1)

            def body(s, par, back, front, late):
                for n in range(N):
                    for half in range(2):
                        dve.wait_ge(da_ready, HALVES * s + 2 * n + half + 1)
                        if half == 0:
                            dve.wait_ge(input_ready, N * s + n + 1)
                        v = state[:, n % RING, 2 * half:2 * half + 2].rearrange("p d t -> p (d t)")
                        dve.tensor_tensor_scan(v, dA[:, half].rearrange("p d t -> p (d t)"), v, 0.0,
                                               ALU.mult, ALU.add).then_inc(scanned, 1)
                        for b in (2 * half, 2 * half + 1):
                            if n > 0:
                                add_state(s, n - 1, b, par)
                            elif back:
                                add_state(s - 1, N - 1, b, 1 - par)
                    if back:
                        back_at(n, s)
                        route_at(n, s)
                    if front:
                        front_at(n, s, 1 - par)

            for n in range(N + 1):
                front_at(n, -1, 0)
            dve.wait_ge(sp_chain, SPC)
            dve.tensor_tensor(delta[:, 0], delta[:, 0], du[:, 0], ALU.add).then_inc(delta_done, 1)
            dve.wait_ge(delta_done, 1)
            dve.wait_ge(silu_done, 1)
            dve.tensor_tensor(du[:, 0], delta[:, 0], xc[:], ALU.mult).then_inc(du_done, 1)
            dve.wait_ge(prep_act, 1)
            dve.tensor_scalar(a_neg[:], a_neg[:], -1.0, None, ALU.mult).then_inc(prep_dve, 1)
            sequences(dve, body)
            q = (SEQS - 1) % 2
            for b in range(TB):
                add_state(SEQS - 1, N - 1, b, q)
            dve.wait_ge(z_done, SEQS)
            for b in range(TB):
                dve.wait_ge(y_added, PIECES * SEQS - TB + b + 1)
                dve.tensor_tensor(y[:, q, b], y[:, q, b], zs[:, q, b], ALU.mult).then_inc(gated, 1)
            for n in range(N):
                back_at(n, SEQS)
                route_at(n, SEQS)

            count = [0]

            def chain(ins):
                count[0] += 1
                ins.then_inc(table_chain, 1)
                dve.wait_ge(table_chain, count[0])

            grid = [P, BLOCKS, E]
            used, n_blocks, end, start, offset, expert = (blocks[:, m] for m in range(6))
            dve.wait_ge(route_chain, RC * SEQS)
            chain(dve.tensor_copy(ends_i[:], base[:, TB:TB + 1]))
            chain(dve.tensor_tensor(used, base[:, TB:TB + 1], region0[:], ALU.subtract))
            chain(dve.tensor_scalar(used_i[:], used, float(P - 1), None, ALU.add))
            chain(dve.tensor_scalar(used_i[:], used_i[:], P.bit_length() - 1, None, ALU.arith_shift_right))
            chain(dve.tensor_copy(n_blocks, used_i[:]))
            chain(dve.tensor_tensor_scan(end[:, 0], ones[:, 0:E], n_blocks[:, 0], 0.0, ALU.mult, ALU.add))
            chain(dve.tensor_tensor(start, end, n_blocks, ALU.subtract))
            chain(dve.scalar_tensor_tensor(offset, start, -float(P), region0[:], ALU.mult, ALU.add))
            numbers = number[:].to_broadcast(grid)
            chain(dve.tensor_tensor(inside[:, 0], numbers, start.to_broadcast(grid), ALU.is_ge))
            chain(dve.tensor_tensor(inside[:, 1], numbers, end.to_broadcast(grid), ALU.is_lt))
            chain(dve.tensor_tensor(inside[:, 0], inside[:, 0], inside[:, 1], ALU.mult))
            chain(dve.tensor_reduce(sums[:, 0], inside[:, 0], X, ALU.add))
            chain(dve.tensor_tensor(inside[:, 1], inside[:, 0], expert.to_broadcast(grid), ALU.mult))
            chain(dve.tensor_reduce(sums[:, 1], inside[:, 1], X, ALU.add))
            chain(dve.tensor_tensor(inside[:, 1], inside[:, 0], offset.to_broadcast(grid), ALU.mult))
            chain(dve.tensor_reduce(sums[:, 2], inside[:, 1], X, ALU.add))
            chain(dve.tensor_scalar(sums[:, 3], sums[:, 0], -float(DUMP - 2 * TOK), float(DUMP - 2 * TOK), ALU.mult, ALU.add))
            chain(dve.tensor_tensor(sums[:, 3], sums[:, 3], sums[:, 2], ALU.add))
            chain(dve.scalar_tensor_tensor(table[:, 0], number[:, :, 0], float(P), sums[:, 3], ALU.mult, ALU.add))
            chain(dve.tensor_copy(table[:, 1], sums[:, 1]))
            chain(dve.tensor_scalar(table[:, 2], number[:, :, 0], float(P), None, ALU.mult))
            assert count[0] == TC1
            shape = [P, SEQS * 2 * TB, E]
            rows_in = routes[:, :, 0:2].bitcast(U32)
            in_region, weighed = (inside[:, m, 0:shape[1]] for m in range(2))
            chain(dve.tensor_copy(end[:, :, 1:E], offset[:, :, 0:E - 1]))
            chain(dve.memset(end[:, :, 0:1], 0.0))
            chain(dve.tensor_tensor(end, offset, end, ALU.subtract))
            dve.wait_ge(route_in, 16)
            chain(dve.tensor_copy(rows_f2, rows_in))
            rows = rows_flat.rearrange("p (r o) -> p r o", o=1)
            chain(dve.tensor_tensor(in_region, rows.to_broadcast(shape), region0[:].to_broadcast(shape), ALU.is_ge))
            chain(dve.tensor_tensor(weighed, in_region, end.to_broadcast(shape), ALU.mult))
            chain(dve.tensor_reduce(sums[:, 0, 0:shape[1]], weighed, X, ALU.add))
            chain(dve.tensor_tensor(rows_out.rearrange("p s c b -> p (s c b)"), rows_flat, sums[:, 0, 0:shape[1]], ALU.subtract))
            assert count[0] == TC1 + TC2

            dve.wait_ge(bias_loaded, 16 * 3)

            def of_expert(bias, e):
                return bias[:, bass.ds(e, 1)].rearrange("p o f -> p (o f)")

            def expert_of(j):
                return dve.value_load(table[0:1, 1, bass.ds(j, 1)], min_val=0, max_val=E - 1)

            def add_biases(j, k, e):
                if not (isinstance(j, int) and j < 2):
                    dve.wait_ge(hid_ready, j - 1)
                    dve.wait_ge(hid_turned, j - 1)
                dve.wait_ge(gate_ready, j + 1)
                dve.tensor_tensor(gate_act[:, k], psum[:, 4 * k + 1], of_expert(g_bias, e), ALU.add).then_inc(gate_biased, 1)
                dve.wait_ge(up_ready, j + 1)
                dve.tensor_tensor(hid[:, k], psum[:, 4 * k + 2], of_expert(u_bias, e), ALU.add).then_inc(up_biased, 1)

            def gate_up(j, k):
                dve.wait_ge(up_biased, j + 1)
                dve.wait_ge(gate_acted, j + 1)
                dve.tensor_tensor(hid[:, k], gate_act[:, k], hid[:, k], ALU.mult).then_inc(hid_ready, 1)

            def copy_result(j, k, e):
                dve.wait_ge(down_ready, j + 1)
                if not (isinstance(j, int) and j < 2):
                    dve.wait_ge(ys_out[k], 16 * (j // 2) if isinstance(j, int) else 8 * (j - k))
                dve.tensor_tensor(ys[:, k], psum[:, 4 * k, DM:2 * DM], of_expert(d_bias, e), ALU.add).then_inc(ys_copied, 1)

            def step(j, k, expert_before):
                e = expert_of(j)
                add_biases(j, k, e)
                gate_up(j, k)
                if not (isinstance(j, int) and j == 0):
                    copy_result(j - 1, 1 - k, expert_of(j - 1) if expert_before is None else expert_before)
                return e

            e = None
            for j in range(FIRST):
                e = step(j, j % 2, e)
            block_loop(dve, step)
            e = step(BLOCKS - 1, (BLOCKS - 1) % 2, None)
            copy_result(BLOCKS - 1, (BLOCKS - 1) % 2, e)

            for s in range(SEQS):
                k = s % 2
                at = LN * s
                dve.wait_ge(fetched_in[k], 16 * 2 * TB * (s // 2 + 1))
                dve.wait_ge(resid_in[k], 16 * (s // 2 + 1))
                for c in range(2):
                    for b in range(TB):
                        if c:
                            dve.wait_ge(summed, 2 * TB * s + b + 1)
                        dve.scalar_tensor_tensor(resid[:, k, b], fetched[:, k, c, b], routes[:, s, 2 + c, b:b + 1], resid[:, k, b],
                                                 ALU.mult, ALU.add).then_inc(summed, 1)
                for b in range(TB):
                    dve.wait_ge(summed, 2 * TB * s + TB + b + 1)
                    dve.bn_stats(stats[:, b], resid[:, k, b]).then_inc(ln2_chain, 1)
                moments(ln2_chain, at)
                dve.wait_ge(rooted, s + 1)
                dve.reciprocal(rstd[:], root[:]).then_inc(rstd2_done, 1)
                dve.wait_ge(rstd2_done, s + 1)
                if s >= 2:
                    dve.wait_ge(out_stored[k], 16 * (s // 2))
                for b in range(TB):
                    dve.tensor_scalar(outs[:, k, b], resid[:, k, b], neg_mean[:, b:b + 1], rstd[:, b:b + 1],
                                      ALU.add, ALU.mult).then_inc(normed, 1)

        @block.tensor
        def _(pe):
            pe.wait_ge(consts, 10)

            def fill(name, s):
                b, earlier = BANK[name], fills_before(name, s)
                if not (isinstance(earlier, int) and earlier == 0):
                    pe.wait_ge(freed[b], earlier)
                return ms[:, b]

            def front_at(n, s, q):
                t = s + 1
                if n == STEP["xt0"]:
                    pe.wait_ge(x_in, 16 * (t + 1))
                    for k in range(KM):
                        bank = fill(f"xt{k}", s)
                        for b in range(TB):
                            ins = pe.transpose(bank[:, b * P:(b + 1) * P], x_sb[:, b, k * P:(k + 1) * P], ident[:])
                        ins.then_inc(filled[BANK[f"xt{k}"]], 1)
                for d in range(DT):
                    if n == STEP[f"in{d}"]:
                        for k in range(KM):
                            wait_copied(pe, f"xt{k}", s)
                        bank = fill(f"in{d}", s)
                        for k in range(KM):
                            ins = pe.matmul(bank, w_in[:, k, d * P:(d + 1) * P], xT[:, k], start=k == 0, stop=k == KM - 1)
                        ins.then_inc(filled[BANK[f"in{d}"]], 1)
                for b in range(TB):
                    if n == STEP[f"z{b}"]:
                        bank = fill(f"z{b}", s)
                        for k in range(KM):
                            ins = pe.matmul(bank, xT[:, k, b * P:(b + 1) * P], w_in[:, k, DI:2 * DI], start=k == 0, stop=k == KM - 1)
                        ins.then_inc(filled[BANK[f"z{b}"]], 1)
                if n == STEP["bc"]:
                    pe.wait_ge(silu_done, t + 1)
                    bank = fill("bc", s)
                    for k in range(DT):
                        ins = pe.matmul(bank[0:1 + 2 * N, :], w_x[:, k], xc[:, k], start=k == 0, stop=k == DT - 1)
                    ins.then_inc(filled[BANK["bc"]], 1)
                if n == STEP["c"]:
                    wait_copied(pe, "bc", s)
                    bank = fill("c", s)
                    for b in range(TB):
                        ins = pe.transpose(bank[:, b * P:(b + 1) * P], bc_sb[:, b * P:(b + 1) * P], ident[:])
                    ins.then_inc(filled[BANK["c"]], 1)
                for b in range(TB):
                    if n == STEP[f"d{b}"]:
                        bank = fill(f"d{b}", s)
                        for k in range(DT):
                            ins = pe.matmul(bank[:, k * P:(k + 1) * P], xc[:, k, b * P:(b + 1) * P], diag_d[:, k], start=True, stop=True)
                        ins.then_inc(filled[BANK[f"d{b}"]], 1)

            def back_at(n, s, q):
                for b in range(TB):
                    if n == STEP[f"g{b}"]:
                        pe.wait_ge(gated, s + b if isinstance(s, int) and s == SEQS else s)
                        bank = fill(f"g{b}", s)
                        for k in range(DT):
                            ins = pe.transpose(bank[:, k * P:(k + 1) * P], y[:, q, b, k * P:(k + 1) * P], ident[:])
                        ins.then_inc(filled[BANK[f"g{b}"]], 1)
                for h in range(2):
                    if n == STEP[f"o{h}"]:
                        for b in range(2 * h, 2 * h + 2):
                            wait_copied(pe, f"g{b}", s)
                        bank = fill(f"o{h}", s)
                        for b in range(2 * h, 2 * h + 2):
                            for k in range(DT):
                                ins = pe.matmul(bank[:, (b % 2) * DM:(b % 2 + 1) * DM], gT[:, b, k], w_out[:, k],
                                                start=k == 0, stop=k == DT - 1)
                        ins.then_inc(filled[BANK[f"o{h}"]], 1)
                if n == STEP["rt0"]:
                    pe.wait_ge(xn_done, TB * s)
                    for k in range(KM):
                        bank = fill(f"rt{k}", s)
                        for b in range(TB):
                            ins = pe.transpose(bank[:, b * P:(b + 1) * P], xn_of(s)[:, b, k * P:(k + 1) * P], ident[:])
                        ins.then_inc(filled[BANK[f"rt{k}"]], 1)
                if n == STEP["lg"]:
                    bank = fill("lg", s)
                    for k in range(KM):
                        wait_copied(pe, f"rt{k}", s)
                    for b in range(TB):
                        for k in range(KM):
                            ins = pe.matmul(bank[:, b * E:(b + 1) * E], xnT[:, k, b * P:(b + 1) * P], w_rt[:, k],
                                            start=k == 0, stop=k == KM - 1)
                    ins.then_inc(filled[BANK["lg"]], 1)
                if n == STEP["pf"]:
                    pe.wait_ge(route_chain, RC * (s - 1) + RC1 + RC2)
                    bank = fill("pf", s)
                    picks = both[:].rearrange("p b e -> p (b e)")
                    pe.matmul(bank[:, 0:TB * E], before[:], picks, start=True, stop=True)
                    ins = pe.matmul(bank[:, TB * E:2 * TB * E], ones[:], picks, start=True, stop=True)
                    ins.then_inc(filled[BANK["pf"]], 1)

            def body(s, par, back, front, late):
                for n in range(N):
                    pe.wait_ge(scanned, HALVES * s + 2 * n + 2)
                    for b in range(TB):
                        at = TB * n + b
                        if at >= 2 or not isinstance(s, int) or s > 0:
                            pe.wait_ge(y_added, PIECES * s + at - 1)
                        for d in range(DT):
                            ins = pe.transpose(hT[:, b % 2, d * P:(d + 1) * P], state[:, n % RING, d, b * P:(b + 1) * P], ident[:])
                        ins.then_inc(ht_ready, 1)
                        if b == 1:
                            if back:
                                back_at(n, s, 1 - par)
                            if front:
                                front_at(n, s, 1 - par)

            for n in range(N):
                if n == STEP["in0"]:
                    pe.wait_ge(w_in_in, 16)
                if n == STEP["bc"]:
                    pe.wait_ge(par_in, 16 * PARAMS)
                    pe.wait_ge(prep_dve, 4 + DT)
                front_at(n, -1, 0)
            sequences(pe, body)
            for n in range(N):
                back_at(n, SEQS, (SEQS - 1) % 2)

            pe.wait_ge(table_chain, TC1)
            pe.wait_ge(w_loaded, 16 * 6)

            def expert_of(j):
                return pe.value_load(table[0:1, 1, bass.ds(j, 1)], min_val=0, max_val=E - 1)

            def turn_rows(j, k):
                pe.wait_ge(xs_in[k], 16 * (j // 2 + 1) if isinstance(j, int) else 8 * (j - k) + 16)
                if not (isinstance(j, int) and j < 4):
                    pe.wait_ge(ys_copied, j - 3)
                for c in range(KM):
                    ins = pe.transpose(psum[:, 4 * k, c * P:(c + 1) * P], xs[:, k, c * P:(c + 1) * P], ident[:])
                ins.then_inc(xs_turned, 1)

            def project(k, e, bank, w, signal):
                for c in range(KM):
                    ins = pe.matmul(psum[:, bank], xsT[:, k, c], w[:, bass.ds(e, 1), c].rearrange("p o f -> p (o f)"),
                                    start=c == 0, stop=c == KM - 1)
                ins.then_inc(signal, 1)

            def gate(j, k, e):
                pe.wait_ge(xs_copied, j + 1)
                if not (isinstance(j, int) and j < 2):
                    pe.wait_ge(gate_biased, j - 1)
                project(k, e, 4 * k + 1, w_gate, gate_ready)

            def up(j, k, e):
                if not (isinstance(j, int) and j < 2):
                    pe.wait_ge(up_biased, j - 1)
                project(k, e, 4 * k + 2, w_up, up_ready)

            def turn_hidden(j, k):
                pe.wait_ge(hid_ready, j + 1)
                if not (isinstance(j, int) and j < 2):
                    pe.wait_ge(hid_copied, j - 1)
                for c in range(FB):
                    ins = pe.transpose(psum[:, 4 * k + 3, c * P:(c + 1) * P], hid[:, k, c * P:(c + 1) * P], ident[:])
                ins.then_inc(hid_turned, 1)

            def down(j, k, e):
                pe.wait_ge(hid_copied, j + 1)
                if isinstance(j, int) and j + 2 >= BLOCKS:
                    pe.wait_ge(xs_copied, BLOCKS)
                else:
                    pe.wait_ge(xs_copied, j + 3)
                if not (isinstance(j, int) and j < 2):
                    pe.wait_ge(ys_copied, j - 1)
                result = psum[:, 4 * k, DM:2 * DM]
                for c in range(FB):
                    ins = pe.matmul(result, hidT[:, k, c], w_down[:, bass.ds(e, 1), c].rearrange("p o m -> p (o m)"),
                                    start=c == 0, stop=c == FB - 1)
                ins.then_inc(down_ready, 1)

            def step(j, k, expert_before, last=False):
                e = expert_of(j)
                gate(j, k, e)
                more = not (isinstance(j, int) and j == 0)
                if more:
                    turn_hidden(j - 1, 1 - k)
                if not last:
                    turn_rows(j + 1, 1 - k)
                up(j, k, e)
                if more:
                    down(j - 1, 1 - k, expert_of(j - 1) if expert_before is None else expert_before)
                return e

            turn_rows(0, 0)
            e = None
            for j in range(FIRST):
                e = step(j, j % 2, e)
            block_loop(pe, step)
            e = step(BLOCKS - 1, (BLOCKS - 1) % 2, None, last=True)
            turn_hidden(BLOCKS - 1, (BLOCKS - 1) % 2)
            down(BLOCKS - 1, (BLOCKS - 1) % 2, e)


_INS = ['L0_attn_x', 'L0_attn_W_in', 'L0_attn_conv_w', 'L0_attn_conv_b', 'L0_attn_W_xproj', 'L0_attn_W_dt',
        'L0_attn_b_dt', 'L0_attn_A_log', 'L0_attn_Dp', 'L0_attn_W_out', 'L0_ffn_router_w', 'L0_ffn_gate_w',
        'L0_ffn_gate_b', 'L0_ffn_up_w', 'L0_ffn_up_b', 'L0_ffn_down_w', 'L0_ffn_down_b']
_OUTS = [((SEQS, T, DM), 'float32')]


def kernel(**inputs):
    import numpy as _np
    import concourse.bacc as _bacc
    from concourse import mybir as _mybir
    from concourse.bass_utils import run_bass_kernel_spmd as _run

    nc = _bacc.Bacc("TRN2", target_bir_lowering=False, num_devices=1)
    arrays, args = {}, []
    for name in _INS:
        a = _np.ascontiguousarray(inputs[name])
        arrays[f"in_{name}_dram"] = a
        args.append(nc.dram_tensor(f"in_{name}_dram", a.shape, _mybir.dt.from_np(a.dtype), kind="ExternalInput").ap())
    for i, (shape, dtype) in enumerate(_OUTS):
        dt = _mybir.dt.from_np(_np.dtype(dtype))
        args.append(nc.dram_tensor(f"out_{i}_dram", shape, dt, kind="ExternalOutput").ap())
    mamba_moe_program(nc, *args)
    r = _run(nc, [arrays], core_ids=[0])
    return r.results[0]["out_0_dram"]
```
